# Optimizing a Trainium2 kernel written in Bass

```python
import numpy as np
import jax
import jax.numpy as jnp

def _softmax(x, axis=-1):
    return jax.nn.softmax(x, axis=axis)
def _gelu(x):
    return jax.nn.gelu(x, approximate=True)
def _silu(x):
    return jax.nn.silu(x)
def _sigmoid(x):
    return jax.nn.sigmoid(x)
def _layernorm(x, axis=-1, eps=1e-5):
    m = jnp.mean(x, axis=axis, keepdims=True)
    v = jnp.var(x, axis=axis, keepdims=True)
    return (x - m) / jnp.sqrt(v + eps)
def _scatter_add(tgt, idx, src, axis=0):
    return tgt.at[idx].add(src)
def _segment_sum(src, seg, n):
    return jax.ops.segment_sum(src, seg, n)

kernel_name = 'mk_dlrm_tower_d1_rec_ca7185'

def setup_inputs(seed: int = 0):
    np.random.seed(seed)
    _w = jnp.asarray
    def _rec_inputs():
        import jax
        import jax.numpy as jnp
        _tk = jax.random.key(seed)
        ids = jnp.stack([jax.random.randint(jax.random.fold_in(_tk, 200 + f), (1024,), 0, v, jnp.int32) for f, v in enumerate([1000, 1000, 100000, 1000000])], axis=1)
        tbl_0 = 0.05 * jax.random.normal(jax.random.fold_in(_tk, 500 + 0), (1000, 4), jnp.float32)
        tbl_1 = 0.05 * jax.random.normal(jax.random.fold_in(_tk, 500 + 1), (1000, 4), jnp.float32)
        tbl_2 = 0.05 * jax.random.normal(jax.random.fold_in(_tk, 500 + 2), (100000, 4), jnp.float32)
        tbl_3 = 0.05 * jax.random.normal(jax.random.fold_in(_tk, 500 + 3), (1000000, 4), jnp.float32)
        _rk = jax.random.fold_in(_tk, 7)
        r_x = 7.22013e-05 + 1.00017 * jax.random.normal(jax.random.fold_in(_rk, 101), (1024, 2048), jnp.float32)
        W_top1 = 0.0197642 * jax.random.normal(jax.random.fold_in(_tk, 801), (2560, 512), jnp.float32)
        W_top2 = 0.0441942 * jax.random.normal(jax.random.fold_in(_tk, 802), (512, 256), jnp.float32)
        W_top3 = 0.0625 * jax.random.normal(jax.random.fold_in(_tk, 803), (256, 1), jnp.float32)
        b_top1 = jnp.zeros((512,), jnp.float32)
        b_top2 = jnp.zeros((256,), jnp.float32)
        return r_x, ids, tbl_0, tbl_1, tbl_2, tbl_3, W_top1, b_top1, W_top2, b_top2, W_top3
    r_x, ids, tbl_0, tbl_1, tbl_2, tbl_3, W_top1, b_top1, W_top2, b_top2, W_top3 = _rec_inputs()
    def _L0_rec_setup():
        import jax, jax.numpy as jnp
        import numpy as np
        B, IN, HID, D, N, OUT = (4096, 2048, 2048, 512, 4, 512)
        H = 8
        HD = D // H

        def _ln(x, g, b):
            m = x.mean(-1, keepdims=True)
            v = ((x - m) ** 2).mean(-1, keepdims=True)
            return (x - m) / jnp.sqrt(v + 1e-05) * g + b
        key = jax.random.key(seed)
        ks = jax.random.split(key, 32)

        def nrm(k, shape, scale=0.02):
            return jax.random.normal(k, shape, jnp.float32) * scale
        inp = {}
        inp['x'] = jax.random.normal(ks[0], (B, IN), jnp.float32)
        inp['strength'] = jax.random.uniform(ks[1], (B, N, N), jnp.float32)
        for t, i in (('er', 2), ('ei', 4)):
            inp[t + '_W1'] = nrm(ks[i], (HID, IN))
            inp[t + '_b1'] = jnp.zeros((HID,), jnp.float32)
            inp[t + '_g1'] = jnp.ones((HID,), jnp.float32)
            inp[t + '_be1'] = jnp.zeros((HID,), jnp.float32)
            inp[t + '_W2'] = nrm(ks[i + 1], (N * D, HID))
            inp[t + '_b2'] = jnp.zeros((N * D,), jnp.float32)
        names = ['Wq_r', 'Wq_i', 'Wk_r', 'Wk_i', 'Wv_r', 'Wv_i', 'Wo_r', 'Wo_i']
        for j, nm in enumerate(names):
            inp[nm] = nrm(ks[6 + j], (D, D))
            inp['b' + nm[1:]] = jnp.zeros((D,), jnp.float32)
        inp['int_Wr'] = jnp.tile(jnp.eye(D, dtype=jnp.float32)[None], (N, 1, 1))
        inp['int_Wi'] = jnp.zeros((N, D, D), jnp.float32)
        inp['meas_Mr'] = nrm(ks[20], (OUT, D), 1.0 / np.sqrt(D))
        inp['meas_Mi'] = nrm(ks[21], (OUT, D), 1.0 / np.sqrt(D))
        inp['post_W'] = nrm(ks[22], (OUT, OUT))
        inp['post_b'] = jnp.zeros((OUT,), jnp.float32)
        inp['post_g'] = jnp.ones((OUT,), jnp.float32)
        inp['post_be'] = jnp.zeros((OUT,), jnp.float32)
        return inp
    _L0_rec_all = _L0_rec_setup()
    _L0_rec_in = {k: v for k, v in _L0_rec_all.items() if k in ('er_W1', 'er_b1', 'er_g1', 'er_be1', 'er_W2', 'er_b2', 'ei_W1', 'ei_b1', 'ei_g1', 'ei_be1', 'ei_W2', 'ei_b2', 'Wq_r', 'bq_r', 'Wq_i', 'bq_i', 'Wk_r', 'bk_r', 'Wk_i', 'bk_i', 'Wv_r', 'bv_r', 'Wv_i', 'bv_i', 'Wo_r', 'bo_r', 'Wo_i', 'bo_i', 'int_Wr', 'int_Wi', 'meas_Mr', 'meas_Mi', 'post_W', 'post_b', 'post_g', 'post_be', )}
    del _L0_rec_all

    return {
        "r_x": r_x,
        "ids": ids,
        "tbl_0": tbl_0,
        "tbl_1": tbl_1,
        "tbl_2": tbl_2,
        "tbl_3": tbl_3,
        "W_top1": W_top1,
        "b_top1": b_top1,
        "W_top2": W_top2,
        "b_top2": b_top2,
        "W_top3": W_top3,
        "L0_rec_er_W1": _L0_rec_in["er_W1"],
        "L0_rec_er_b1": _L0_rec_in["er_b1"],
        "L0_rec_er_g1": _L0_rec_in["er_g1"],
        "L0_rec_er_be1": _L0_rec_in["er_be1"],
        "L0_rec_er_W2": _L0_rec_in["er_W2"],
        "L0_rec_er_b2": _L0_rec_in["er_b2"],
        "L0_rec_ei_W1": _L0_rec_in["ei_W1"],
        "L0_rec_ei_b1": _L0_rec_in["ei_b1"],
        "L0_rec_ei_g1": _L0_rec_in["ei_g1"],
        "L0_rec_ei_be1": _L0_rec_in["ei_be1"],
        "L0_rec_ei_W2": _L0_rec_in["ei_W2"],
        "L0_rec_ei_b2": _L0_rec_in["ei_b2"],
        "L0_rec_Wq_r": _L0_rec_in["Wq_r"],
        "L0_rec_bq_r": _L0_rec_in["bq_r"],
        "L0_rec_Wq_i": _L0_rec_in["Wq_i"],
        "L0_rec_bq_i": _L0_rec_in["bq_i"],
        "L0_rec_Wk_r": _L0_rec_in["Wk_r"],
        "L0_rec_bk_r": _L0_rec_in["bk_r"],
        "L0_rec_Wk_i": _L0_rec_in["Wk_i"],
        "L0_rec_bk_i": _L0_rec_in["bk_i"],
        "L0_rec_Wv_r": _L0_rec_in["Wv_r"],
        "L0_rec_bv_r": _L0_rec_in["bv_r"],
        "L0_rec_Wv_i": _L0_rec_in["Wv_i"],
        "L0_rec_bv_i": _L0_rec_in["bv_i"],
        "L0_rec_Wo_r": _L0_rec_in["Wo_r"],
        "L0_rec_bo_r": _L0_rec_in["bo_r"],
        "L0_rec_Wo_i": _L0_rec_in["Wo_i"],
        "L0_rec_bo_i": _L0_rec_in["bo_i"],
        "L0_rec_int_Wr": _L0_rec_in["int_Wr"],
        "L0_rec_int_Wi": _L0_rec_in["int_Wi"],
        "L0_rec_meas_Mr": _L0_rec_in["meas_Mr"],
        "L0_rec_meas_Mi": _L0_rec_in["meas_Mi"],
        "L0_rec_post_W": _L0_rec_in["post_W"],
        "L0_rec_post_b": _L0_rec_in["post_b"],
        "L0_rec_post_g": _L0_rec_in["post_g"],
        "L0_rec_post_be": _L0_rec_in["post_be"],
    }

def reference(r_x, ids, tbl_0, tbl_1, tbl_2, tbl_3, W_top1, b_top1, W_top2, b_top2, W_top3, L0_rec_er_W1, L0_rec_er_b1, L0_rec_er_g1, L0_rec_er_be1, L0_rec_er_W2, L0_rec_er_b2, L0_rec_ei_W1, L0_rec_ei_b1, L0_rec_ei_g1, L0_rec_ei_be1, L0_rec_ei_W2, L0_rec_ei_b2, L0_rec_Wq_r, L0_rec_bq_r, L0_rec_Wq_i, L0_rec_bq_i, L0_rec_Wk_r, L0_rec_bk_r, L0_rec_Wk_i, L0_rec_bk_i, L0_rec_Wv_r, L0_rec_bv_r, L0_rec_Wv_i, L0_rec_bv_i, L0_rec_Wo_r, L0_rec_bo_r, L0_rec_Wo_i, L0_rec_bo_i, L0_rec_int_Wr, L0_rec_int_Wi, L0_rec_meas_Mr, L0_rec_meas_Mi, L0_rec_post_W, L0_rec_post_b, L0_rec_post_g, L0_rec_post_be):
    import jax
    import jax.numpy as jnp
    def _L0_rec_ref(x, strength, er_W1, er_b1, er_g1, er_be1, er_W2, er_b2, ei_W1, ei_b1, ei_g1, ei_be1, ei_W2, ei_b2, Wq_r, bq_r, Wq_i, bq_i, Wk_r, bk_r, Wk_i, bk_i, Wv_r, bv_r, Wv_i, bv_i, Wo_r, bo_r, Wo_i, bo_i, int_Wr, int_Wi, meas_Mr, meas_Mi, post_W, post_b, post_g, post_be):
        import jax, jax.numpy as jnp
        import numpy as np
        B, IN, HID, D, N, OUT = (4096, 2048, 2048, 512, 4, 512)
        H = 8
        HD = D // H

        def _ln(x, g, b):
            m = x.mean(-1, keepdims=True)
            v = ((x - m) ** 2).mean(-1, keepdims=True)
            return (x - m) / jnp.sqrt(v + 1e-05) * g + b
        Bsz = x.shape[0]

        def enc(W1, b1, g, be, W2, b2):
            h = jax.nn.gelu(_ln(x @ W1.T + b1, g, be), approximate=False)
            return (h @ W2.T + b2).reshape(Bsz, N, D)
        sr = enc(er_W1, er_b1, er_g1, er_be1, er_W2, er_b2)
        si = enc(ei_W1, ei_b1, ei_g1, ei_be1, ei_W2, ei_b2)

        def heads(t):
            return t.reshape(Bsz, N, H, HD).transpose(0, 2, 1, 3)
        qr = heads(sr @ Wq_r.T + bq_r)
        qi = heads(si @ Wq_i.T + bq_i)
        kr = heads(sr @ Wk_r.T + bk_r)
        ki = heads(si @ Wk_i.T + bk_i)
        vr = heads(sr @ Wv_r.T + bv_r)
        vi = heads(si @ Wv_i.T + bv_i)
        ar = jnp.einsum('bhnd,bhmd->bhnm', qr, kr) + jnp.einsum('bhnd,bhmd->bhnm', qi, ki)
        ai = jnp.einsum('bhnd,bhmd->bhnm', qi, kr) - jnp.einsum('bhnd,bhmd->bhnm', qr, ki)
        mag = jnp.sqrt(ar ** 2 + ai ** 2 + 1e-08) * HD ** (-0.5)
        w = jax.nn.softmax(mag, axis=-1)
        out_r = jnp.einsum('bhnm,bhmd->bhnd', w, vr).transpose(0, 2, 1, 3).reshape(Bsz, N, D)
        out_i = jnp.einsum('bhnm,bhmd->bhnd', w, vi).transpose(0, 2, 1, 3).reshape(Bsz, N, D)
        attn_r = out_r @ Wo_r.T + bo_r
        attn_i = out_i @ Wo_i.T + bo_i
        R = jnp.einsum('bnd,ned->bne', attn_r, int_Wr) - jnp.einsum('bnd,ned->bne', attn_i, int_Wi)
        I = jnp.einsum('bnd,ned->bne', attn_r, int_Wi) + jnp.einsum('bnd,ned->bne', attn_i, int_Wr)
        Ri, Ii = (R[:, :, None, :], I[:, :, None, :])
        Rj, Ij = (R[:, None, :, :], I[:, None, :, :])
        phase = jnp.arctan2(Ii * Rj - Ri * Ij, Ri * Rj + Ii * Ij)
        f = jnp.cos(phase) * strength[..., None]
        sup_r = jnp.einsum('bijd,bjd->bd', f, R)
        sup_i = jnp.einsum('bijd,bjd->bd', f, I)
        norm = jnp.sqrt(jnp.sum(sup_r ** 2 + sup_i ** 2, axis=-1, keepdims=True) + 1e-08)
        sup_r = sup_r / norm
        sup_i = sup_i / norm
        mr = sup_r @ meas_Mr.T - sup_i @ meas_Mi.T
        mi = sup_r @ meas_Mi.T + sup_i @ meas_Mr.T
        amp = jnp.sqrt(mr ** 2 + mi ** 2)
        out = jax.nn.gelu(_ln(amp @ post_W.T + post_b, post_g, post_be), approximate=False)
        return out

    e = jnp.stack([tbl_0[ids[:, 0]], tbl_1[ids[:, 1]], tbl_2[ids[:, 2]], tbl_3[ids[:, 3]]], axis=1)
    z = _L0_rec_ref(r_x, e, L0_rec_er_W1, L0_rec_er_b1, L0_rec_er_g1, L0_rec_er_be1, L0_rec_er_W2, L0_rec_er_b2, L0_rec_ei_W1, L0_rec_ei_b1, L0_rec_ei_g1, L0_rec_ei_be1, L0_rec_ei_W2, L0_rec_ei_b2, L0_rec_Wq_r, L0_rec_bq_r, L0_rec_Wq_i, L0_rec_bq_i, L0_rec_Wk_r, L0_rec_bk_r, L0_rec_Wk_i, L0_rec_bk_i, L0_rec_Wv_r, L0_rec_bv_r, L0_rec_Wv_i, L0_rec_bv_i, L0_rec_Wo_r, L0_rec_bo_r, L0_rec_Wo_i, L0_rec_bo_i, L0_rec_int_Wr, L0_rec_int_Wi, L0_rec_meas_Mr, L0_rec_meas_Mi, L0_rec_post_W, L0_rec_post_b, L0_rec_post_g, L0_rec_post_be)
    z = z.reshape(z.shape[0], -1)
    h = jnp.concatenate([z, r_x], axis=1)
    h = jnp.maximum(h @ W_top1 + b_top1, 0.0)
    h = jnp.maximum(h @ W_top2 + b_top2, 0.0)
    y = h @ W_top3
    return y


_drawn_inputs = setup_inputs


def setup_inputs(seed=0):
    import zlib

    import numpy as np

    out = dict(_drawn_inputs(seed))
    spreads = {'b_top1': (0.0, 0.1),
     'b_top2': (0.0, 0.1),
     'L0_rec_er_b1': (0.0, 0.8),
     'L0_rec_er_g1': (1.0, 0.6),
     'L0_rec_er_be1': (0.0, 0.8),
     'L0_rec_er_b2': (0.0, 0.8),
     'L0_rec_ei_b1': (0.0, 0.8),
     'L0_rec_ei_g1': (1.0, 0.6),
     'L0_rec_ei_be1': (0.0, 0.8),
     'L0_rec_ei_b2': (0.0, 0.8),
     'L0_rec_bq_r': (0.0, 0.8),
     'L0_rec_bq_i': (0.0, 0.8),
     'L0_rec_bk_r': (0.0, 0.8),
     'L0_rec_bk_i': (0.0, 0.8),
     'L0_rec_bv_r': (0.0, 0.1),
     'L0_rec_bv_i': (0.0, 0.1),
     'L0_rec_bo_r': (0.0, 0.1),
     'L0_rec_bo_i': (0.0, 0.1),
     'L0_rec_int_Wi': (0.0, 0.1),
     'L0_rec_post_b': (0.0, 0.1),
     'L0_rec_post_g': (1.0, 0.2),
     'L0_rec_post_be': (0.0, 0.1)}
    factors = {'L0_rec_Wq_r': 8.0, 'L0_rec_Wq_i': 8.0, 'L0_rec_Wk_r': 8.0, 'L0_rec_Wk_i': 8.0}
    for name, (base, spread) in spreads.items():
        noise = np.random.default_rng([zlib.crc32(name.encode()), seed]).standard_normal(out[name].shape)
        drawn = base * np.exp(spread * noise) if base else spread * noise
        out[name] = jnp.asarray(drawn.astype(out[name].dtype))
    for name, factor in factors.items():
        out[name] = (out[name] * factor).astype(out[name].dtype)
    return out
```

```python
from contextlib import ExitStack

import concourse.bass as bass
from concourse import mybir

F32 = mybir.dt.float32
F32R = mybir.dt.float32r
I32 = mybir.dt.int32
BF16 = mybir.dt.bfloat16
U8 = mybir.dt.uint8
ACT = mybir.ActivationFunctionType
ALU = mybir.AluOpType
AX = mybir.AxisListType

P = 128
BATCH, IN, HID, D, N = 1024, 2048, 2048, 512, 4
HEADS, HD = 8, 64
HALF = 512
HALVES = BATCH // HALF
KC = IN // P
C = D // P
UC = 8
UNIT = UC * P
BLOCKS = {"W1r": 16, "W1i": 16, "W2r": 16, "top": 4, "W2i": 16}
FIRST_UNIT = {"W1r": 0, "W1i": 32, "W2r": 64, "W2i": 96, "top": 128}
JOBS = ["W1r", "W1i", "W2r", "top", "W2i"]
START = {j: sum(BLOCKS[k] for k in JOBS[:n]) for n, j in enumerate(JOBS)}
PER_HALF = sum(BLOCKS.values())
X_UNITS = 8
X_STEPS = range(2, 6)
LN_EPS = 1e-5
TILES = BATCH // P


PARAM = {}
_at = 0
for _name, _n in (("r_b1", 16), ("r_g1", 16), ("r_be1", 16), ("i_b1", 16), ("i_g1", 16), ("i_be1", 16),
                  ("r_b2", 16), ("i_b2", 16), ("top1", 4), ("q_r", 4), ("q_i", 4), ("k_r", 4), ("k_i", 4),
                  ("v_r", 4), ("v_i", 4), ("o_r", 4), ("o_i", 4),
                  ("post_b", 4), ("post_g", 4), ("post_be", 4), ("top2", 2), ("w3", 2)):
    PARAM[_name] = _at
    _at += _n
PARAMS = _at



def act_bias(params, name, index):
    return params[:, bass.ds(PARAM[name] + index, 1)]


def pair_of(half, job, b, with_x=0):
    return X_UNITS // 2 + half * (PER_HALF + X_UNITS // 2) + START[job] + b + with_x


def block_of(half, job, b):
    return half * PER_HALF + START[job] + b


def w2_block_of(half, job, b):
    return half * 32 + (16 if job == "W2i" else 0) + b


def w1_block_of(half, job, b):
    return half * 32 + (16 if job == "W1i" else 0) + b


def before(half, job, s):
    if not isinstance(s, int) or s >= 2:
        return half, job, s - 2
    n = JOBS.index(job)
    if n:
        return half, JOBS[n - 1], BLOCKS[JOBS[n - 1]] - 2 + s
    return (half - 1, JOBS[-1], BLOCKS[JOBS[-1]] - 2 + s) if half else None


def after(half, job, s):
    if not isinstance(s, int) or s + 1 < BLOCKS[job]:
        return half, job, s + 1
    n = JOBS.index(job)
    if n + 1 < len(JOBS):
        return half, JOBS[n + 1], 0
    return (half + 1, JOBS[0], 0) if half + 1 < HALVES else None


def x_pairs(job, b):
    if job != "W2i" or (isinstance(b, int) and b <= 3):
        return 0
    return min(b - 3, 4) if isinstance(b, int) else 4


def steps(eng, job, do):
    head = 6 if job == "W2i" else 4
    for b in range(head):
        do(b, b % 4)
    with eng.Fori(0, 2) as i:
        for k in range(4):
            do(i * 4 + (head + k), (head + k) % 4)
    for b in range(head + 8, 16):
        do(b, b % 4)


def encoder_loads(nc, sp, io, m, s):
    def pair(q, src, first):
        for k in range(2):
            if not isinstance(q, int) or q >= 1:
                sp.wait_ge(s.lo_done, q * 2 + (k - 1))
            sp.dma_start(m.raw[:, k, :], src[first + k]).then_inc(s.raw_loaded[k], 16)

    for q in range(4):
        pair(q, io.x_units, 2 * q)
    for half in range(HALVES):
        for job in JOBS:
            def load(b, with_x):
                pair(pair_of(half, job, b, with_x), io.w_units, b * 2 + FIRST_UNIT[job])

            if job != "W2i":
                with sp.Fori(0, BLOCKS[job]) as b:
                    load(b, 0)
                continue
            with sp.Fori(0, 4) as b:
                load(b, 0)
            for n in range(4):
                pair(pair_of(half, job, 4 + n, n), io.x_units, X_UNITS * (half + 1) + 2 * n)
                if n < 3:
                    load(4 + n, n + 1)
            with sp.Fori(7, 16) as b:
                load(b, 4)


def cut_hi(nc, act, m, s, q, dst, k):
    act.wait_ge(s.raw_loaded[k], (q + 1) * 16)
    nc.scalar.copy(dst[0], m.raw[:, k, :]).then_inc(s.hi_done, 1)


def cut_lo(nc, dve, m, s, q, dst, k):
    dve.wait_ge(s.hi_done, q * 2 + (k + 1))
    nc.vector.tensor_tensor(dst[1], m.raw[:, k, :], dst[0].bitcast(F32), ALU.subtract).then_inc(s.lo_done, 1)


def w_slot(m, parity, k):
    return [m.ws[:, parity, k, part, :] for part in range(2)]


def x_slot(m, n):
    return [m.x[:, part, bass.ts(n, UNIT)] for part in range(2)]


def encoder_scalar(nc, act, io, m, s):
    for q in range(4):
        for k in range(2):
            cut_hi(nc, act, m, s, q, x_slot(m, 2 * q + k), k)
    for k in range(2):
        cut_hi(nc, act, m, s, 4, w_slot(m, 0, k), k)

    for half in range(HALVES):
        for job in JOBS:
            def step(b, phase, between=None):
                nxt = after(half, job, b)
                if nxt:
                    w = block_of(*nxt)
                    if not isinstance(w, int) or w >= 2:
                        act.wait_ge(s.block_done, w - 1)
                    q = pair_of(nxt[0], nxt[1], nxt[2], x_pairs(nxt[1], nxt[2]))
                    for k in range(2):
                        cut_hi(nc, act, m, s, q, w_slot(m, (phase + 1) % 2, k), k)
                if between:
                    between()
                old = before(half, job, b)
                if old:
                    take_out(old, (phase - 2) % 4)
                if job == "W2i" and isinstance(b, int) and b in X_STEPS:
                    n = b - X_STEPS[0]
                    for k in range(2):
                        cut_hi(nc, act, m, s, pair_of(half, job, b + 2, n), x_slot(m, 2 * n + k), k)

            def take_out(old, bank):
                oh, oj, ob = old
                acc = m.acc[:, bank, :]
                w = block_of(oh, oj, ob)
                act.wait_ge(s.block_done, w + 1)
                if oj in ("W1r", "W1i"):
                    bias = act_bias(m.params, oj[2] + "_b1", ob)
                    u = w1_block_of(oh, oj, ob)
                    if oh or oj == "W1i":
                        act.wait_ge(s.norm_lo, u - 15)
                    if not isinstance(u, int) or u % 16 >= 2:
                        act.wait_ge(s.sq_added, u - 1)
                    elif u >= 16:
                        act.wait_ge(s.rstd_done, u // 16)
                        if u == 32:
                            act.wait_ge(s.stored, 32 * 32)
                    nc.scalar.activation(m.pre[:, bass.ts(ob, HALF)], acc, ACT.Identity, bias=bias).then_inc(s.pre_done, 1)
                    nc.scalar.activation(m.tmp[:, bank % 2, :], acc, ACT.Square, bias=bias).then_inc(s.evac_act, 1)
                elif oj == "top":
                    t = oh * 4 + ob
                    act.wait_ge(s.stored, 32 * w2_block_of(oh, "W2i", 0))
                    if t >= 1:
                        act.wait_ge(s.stored_top, 16 * t)
                    nc.scalar.activation(m.tmp[:, 0, :], acc, ACT.Identity,
                                         bias=act_bias(m.params, "top1", ob)).then_inc(s.evac_act, 1)
                else:
                    v = w2_block_of(oh, oj, ob)
                    if oj == "W2i" and isinstance(ob, int) and ob == 0:
                        act.wait_ge(s.stored_top, 16 * 4 * (oh + 1))
                    if not isinstance(v, int) or v >= 1:
                        act.wait_ge(s.stored, v * 32)
                    if oj == "W2r" and isinstance(ob, int) and ob == 0:
                        act.wait_ge(s.rstd_done, 2 * oh + 2)
                    nc.scalar.activation(m.tmp[:, 0, :].bitcast(F32R), acc, ACT.Identity,
                                         bias=act_bias(m.params, oj[2] + "_b2", ob)).then_inc(s.evac_act, 1)

            def normalise(b, n):
                enc = "r" if job == "W1i" else "i"
                act.wait_ge(s.block_done, block_of(half, "top" if job == "top" else "W1r", 0))
                for j in range(2):
                    act.wait_ge(s.norm_scaled, n + (j + 1))
                    cols = bass.ts(b + j, HALF)
                    nc.scalar.activation(m.pre[:, cols], m.pre[:, cols], ACT.Gelu,
                                         bias=act_bias(m.params, enc + "_be1", b + j),
                                         scale=act_bias(m.params, enc + "_g1", b + j)).then_inc(s.gelu_done, 1)
                    act.wait_ge(s.gelu_done, n + (j + 1))
                    nc.scalar.copy(m.h[:, 0, cols], m.pre[:, cols]).then_inc(s.norm_hi, 1)

            def deviation(r):
                act.wait_ge(s.means_done, r + 1)
                nc.scalar.activation(m.tmp[:, 0, :], m.mean, ACT.Square).then_inc(s.mean_sq, 1)
                act.wait_ge(s.var_done, r + 1)
                nc.scalar.activation(m.tmp[:, 0, :], m.tmp[:, 1, :], ACT.Sqrt).then_inc(s.std_done, 1)

            job_steps(act, half, job, step, normalise, deviation)
    for b in (14, 15):
        take_out((HALVES - 1, "W2i", b), b % 4)


def job_steps(eng, half, job, step, normalise, deviation):
    if job == "W1i":
        first = half * 32
        step(0, 0)
        step(1, 1)
        deviation(2 * half)
        for b in range(2, 16):
            step(b, b % 4, (lambda: normalise(2 * (b - 2), first + 2 * (b - 2))) if b < 10 else None)
    elif job == "top":
        first = half * 32 + 16
        for b in range(4):
            step(b, b)
            with eng.Fori(0, 2) as i:
                normalise(i * 2 + 4 * b, i * 2 + (first + 4 * b))
    elif job == "W2r":
        def with_deviation(b, phase):
            step(b, phase)
            if isinstance(b, int) and b == 1:
                deviation(2 * half + 1)

        steps(eng, job, with_deviation)
    else:
        steps(eng, job, step)


def encoder_vector(nc, dve, io, m, s):
    for q in range(4):
        for k in range(2):
            cut_lo(nc, dve, m, s, q, x_slot(m, 2 * q + k), k)
    for k in range(2):
        cut_lo(nc, dve, m, s, 4, w_slot(m, 0, k), k)

    for half in range(HALVES):
        for job in JOBS:
            def step(b, phase, between=None):
                nxt = after(half, job, b)
                if nxt:
                    q = pair_of(nxt[0], nxt[1], nxt[2], x_pairs(nxt[1], nxt[2]))
                    for k in range(2):
                        cut_lo(nc, dve, m, s, q, w_slot(m, (phase + 1) % 2, k), k)
                if between:
                    between()
                old = before(half, job, b)
                if old:
                    take_out(old, (phase - 2) % 4)
                if job == "W2i" and isinstance(b, int) and b in X_STEPS:
                    n = b - X_STEPS[0]
                    for k in range(2):
                        cut_lo(nc, dve, m, s, pair_of(half, job, b + 2, n), x_slot(m, 2 * n + k), k)

            def take_out(old, bank):
                oh, oj, ob = old
                if oj == "top":
                    return
                w = block_of(oh, oj, ob)
                if oj in ("W1r", "W1i"):
                    u = w1_block_of(oh, oj, ob)
                    start = isinstance(ob, int) and ob == 0
                    dve.wait_ge(s.pre_done, u + 1)
                    pre, sq = m.pre[:, bass.ts(ob, HALF)], m.tmp[:, bank % 2, :]
                    if start:
                        nc.vector.tensor_copy(m.sums, pre).then_inc(s.pre_added, 1)
                    else:
                        dve.wait_ge(s.pre_added, u)
                        nc.vector.tensor_tensor(m.sums, m.sums, pre, ALU.add).then_inc(s.pre_added, 1)
                    dve.wait_ge(s.evac_act, w + 1)
                    if start:
                        nc.vector.tensor_copy(m.sums_sq, sq).then_inc(s.sq_added, 1)
                    else:
                        dve.wait_ge(s.sq_added, u)
                        nc.vector.tensor_tensor(m.sums_sq, m.sums_sq, sq, ALU.add).then_inc(s.sq_added, 1)
                    if isinstance(ob, int) and ob == 15:
                        r = u // 16
                        dve.wait_ge(s.pre_added, u + 1)
                        dve.wait_ge(s.sq_added, u + 1)
                        nc.vector.tensor_copy(m.tmp[:, 0, :], m.sums).then_inc(s.sums_ready, 1)
                        nc.vector.tensor_copy(m.tmp[:, 1, :], m.sums_sq).then_inc(s.sums_ready, 1)
                else:
                    v = w2_block_of(oh, oj, ob)
                    dve.wait_ge(s.evac_act, w + 1)
                    if not isinstance(v, int) or v >= 1:
                        dve.wait_ge(s.stored, v * 32)
                    nc.vector.scalar_tensor_tensor(
                        out=m.tmp[:, 1, :].bitcast(F32R), in0=m.acc[:, bank, :],
                        scalar=act_bias(m.params, oj[2] + "_b2", ob), in1=m.tmp[:, 0, :],
                        op0=ALU.add, op1=ALU.subtract).then_inc(s.evac_dve, 1)

            def normalise(b, n):
                for j in range(2):
                    cols = bass.ts(b + j, HALF)
                    nc.vector.tensor_tensor(m.pre[:, cols], m.pre[:, cols], m.mean, ALU.subtract).then_inc(s.norm_centred, 1)
                    dve.wait_ge(s.norm_centred, n + (j + 1))
                    nc.vector.tensor_tensor(m.pre[:, cols], m.pre[:, cols], m.rstd, ALU.mult).then_inc(s.norm_scaled, 1)
                for j in range(2):
                    cols = bass.ts(b + j, HALF)
                    dve.wait_ge(s.norm_hi, n + (j + 1))
                    nc.vector.tensor_tensor(m.h[:, 1, cols], m.pre[:, cols], m.h[:, 0, cols].bitcast(F32),
                                            ALU.subtract).then_inc(s.norm_lo, 1)

            def deviation(r):
                dve.wait_ge(s.mean_sq, r + 1)
                nc.vector.tensor_tensor(m.tmp[:, 1, :], m.rstd, m.tmp[:, 0, :], ALU.subtract).then_inc(s.var_raw, 1)
                dve.wait_ge(s.var_raw, r + 1)
                nc.vector.tensor_scalar(m.tmp[:, 1, :], m.tmp[:, 1, :], 0.0, LN_EPS, ALU.max, ALU.add).then_inc(s.var_done, 1)
                dve.wait_ge(s.std_done, r + 1)
                nc.vector.reciprocal(m.rstd, m.tmp[:, 0, :]).then_inc(s.rstd_done, 1)
                dve.wait_ge(s.rstd_done, r + 1)

            job_steps(dve, half, job, step, normalise, deviation)
    for b in (14, 15):
        take_out((HALVES - 1, "W2i", b), b % 4)


def product(nc, out, stationary, moving, start, stop):
    nc.tensor.matmul(out, stationary[0], moving[0], start=start, stop=False)
    nc.tensor.matmul(out, stationary[0], moving[1], start=False, stop=False)
    return nc.tensor.matmul(out, stationary[1], moving[0], start=False, stop=stop)


def encoder_tensor(nc, pe, io, m, s):
    def means(r):
        pe.wait_ge(s.sums_ready, 2 * r + 2)
        nc.tensor.matmul(m.mean, m.table[:, :], m.tmp[:, 0, :], start=True, stop=True)
        nc.tensor.matmul(m.rstd, m.table[:, :], m.tmp[:, 1, :], start=True, stop=True).then_inc(s.means_done, 1)

    for half in range(HALVES):
        for job in JOBS:
            src = m.h if job[:2] == "W2" else m.x

            def compute(b, phase, with_x):
                w = block_of(half, job, b)
                if not isinstance(b, int) or b >= 4:
                    free = (half, job, b - 4)
                else:
                    free = (half, job, b)
                    n = JOBS.index(job)
                    prev = JOBS[n - 1]
                    free = (half if n else half - 1, prev, BLOCKS[prev] - 4 + b)
                if free[0] >= 0:
                    if free[1][:2] == "W2":
                        pe.wait_ge(s.evac_dve, w2_block_of(*free) + 1)
                    else:
                        pe.wait_ge(s.evac_act, block_of(*free) + 1)
                q = pair_of(half, job, b, with_x)
                for k in range(2):
                    pe.wait_ge(s.lo_done, q * 2 + (k + 1))
                    for c in range(UC):
                        wh, wl = (m.ws[:, phase % 2, k, part, bass.ts(c, P)] for part in range(2))
                        cols = bass.ts(UC * k + c, HALF)
                        last = product(nc, m.acc[:, phase, :], (wh, wl), (src[:, 0, cols], src[:, 1, cols]),
                                       k == 0 and c == 0, k == 1 and c == UC - 1)
                last.then_inc(s.block_done, 1)

            if job[:2] == "W2":
                pe.wait_ge(s.norm_lo, half * 32 + (32 if job == "W2i" else 16))
            if job == "top":
                for b in range(4):
                    compute(b, b, 0)
                continue
            head = 8 if job == "W2i" else 4
            for b in range(head):
                compute(b, b % 4, x_pairs(job, b))
                if b == 1 and job in ("W1i", "W2r"):
                    means(half * 2 + (job == "W2r"))
            with pe.Fori(0, (16 - head) // 4) as i:
                for k in range(4):
                    compute(i * 4 + (head + k), k, 4 if job == "W2i" else 0)


def encoder_stores(nc, pool, io, m, s):
    for half in range(HALVES):
        toks = bass.ds(half * HALF, HALF)

        def store(ri, b):
            v = half * 32 + ri * 16 + b
            pool.wait_ge(s.evac_dve, v + 1)
            for part in range(2):
                pool.dma_start(io.s_scr[ri, part, :, :, :, toks].rearrange("n c p r -> (n c) p r")[b], m.tmp[:, part, :].bitcast(F32R)).then_inc(s.stored, 16)

        with pool.Fori(0, 16) as b:
            store(0, b)
        for b in range(4):
            pool.wait_ge(s.evac_act, block_of(half, "top", b) + 1)
            pool.dma_start(io.top_scr[b, :, toks], m.tmp[:, 0, :]).then_inc(s.stored_top, 16)
        with pool.Fori(0, 16) as b:
            store(1, b)



QK_BUFS = 2
QR, QI, KI, KR, NKI = range(5)
MATRICES = [(0, QR, "q_r"), (1, QI, "q_i"), (2, KR, "k_r"), (3, KI, "k_i")]
PAIRS = HEADS // 2
STEPS_Q = TILES * PAIRS
GROUPS = 4


def tile_view(m, buf):
    return m.h[:, buf, :].rearrange("p (a b c w) -> p a b c w", a=2, b=2, c=C)


def load_tile(sp, m, scr, buf, t, sem):
    for ri in range(2):
        for part in range(2):
            for c in range(C):
                sp.dma_start(tile_view(m, buf)[:, ri, part, c, :].rearrange("p (n r) -> p n r", n=N).bitcast(F32),
                             scr[ri, part, :, c, :, bass.ts(t, P)].rearrange("n p r -> p n r")).then_inc(sem, 16)


TILE_DMAS = 2 * 2 * C


def rolled(eng, rounds, unroll, do, ahead=0):
    for k in range(unroll):
        do(0, k, True)
    with eng.Fori(1, rounds - 1) as i:
        for k in range(unroll):
            do(i, k, True)
    for k in range(unroll):
        do(rounds - 1, k, k + ahead < unroll)


def from_step(i, k, n):
    return k >= n or not isinstance(i, int) or i > 0


def following(i, k, unroll):
    return (i, k + 1) if k + 1 < unroll else (i + 1, 0)


def scores_sync(nc, sp, io, m, s):
    sp.wait_ge(s.stored, 32 * 32 * HALVES)
    sp.wait_ge(s.block_done, HALVES * PER_HALF)
    for t in range(2):
        load_tile(sp, m, io.s_scr, t, t, s.tile_loaded[t])
    with sp.Fori(1, TILES // 2) as i:
        for k in range(2):
            sp.wait_ge(s.projected, i * 32 + (16 * k - 16))
            load_tile(sp, m, io.s_scr, k, i * 2 + k, s.tile_loaded[k])


def scores_tensor(nc, pe, io, m, s):
    def project(i, k):
        j, buf = k % PAIRS, k // PAIRS
        view = tile_view(m, buf)
        if j == 0:
            pe.wait_ge(s.tile_loaded[buf], i * (16 * TILE_DMAS) + 16 * TILE_DMAS)
        for mat, slot, _ in MATRICES:
            if from_step(i, k, 1):
                pe.wait_ge(s.qk_lo, i * 32 + (4 * k + mat - 3))
            for c in range(C):
                st = [m.x[:, part, bass.ds(mat * C * D + c * D + j * P, P)] for part in range(2)]
                mv = [view[:, mat % 2, part, c, :].rearrange("p (n g r) -> p g n r", n=N, g=GROUPS) for part in range(2)]
                last = product(nc, m.acc[:, mat, :], st, mv, c == 0, c == C - 1)
            last.then_inc(s.projected, 1)

    def score(i, k):
        buf = k % QK_BUFS
        pe.wait_ge(s.qk_lo, i * 32 + (4 * k + 4))
        pe.wait_ge(s.nki_done, i * 8 + (k + 1))
        for gp in range(2):
            if from_step(i, k, 1):
                pe.wait_ge(s.masked, i * 32 + (4 * k + 2 * gp - 2))
            for g2 in range(2):
                group = bass.ts(2 * gp + g2, P)
                for a, (slot, first) in enumerate(((QR, KR), (QI, KI))):
                    for b, (ps, pm) in enumerate(((0, 0), (0, 1), (1, 0))):
                        for hh in range(2):
                            part = slice(64 * hh, 64 * hh + 64)
                            st = m.qk[part, buf, slot, ps, group]
                            mv = m.qk[part, buf, first:first + 2, pm, group]
                            last = nc.tensor.matmul(m.stat[:, 2 * gp + hh, bass.ts(g2, 256)], st, mv,
                                                    start=(a == 0 and b == 0), stop=(a == 1 and b == 2))
                            if g2 == 1 and a == 1 and b == 2:
                                last.then_inc(s.scored, 1)

    pe.wait_ge(s.lo_done, 2 * pair_of(HALVES, "W1r", 0))
    pe.wait_ge(s.evac_dve, 32 * HALVES)
    project(0, 0)

    def step(i, k, more):
        if more:
            project(*following(i, k, 8))
        score(i, k)

    rolled(pe, STEPS_Q // 8, 8, step, 1)


def qk_scalar(nc, act, io, m, s):
    act.wait_ge(s.norm_lo, 32 * HALVES)
    act.wait_ge(s.block_done, HALVES * PER_HALF)
    act.wait_ge(s.stored, 32 * 32 * HALVES)

    def hi(i, k):
        buf = k % QK_BUFS
        if from_step(i, k, 2):
            act.wait_ge(s.scored, i * 32 + (4 * k - 4))
        for mat, slot, name in MATRICES:
            act.wait_ge(s.projected, i * 32 + (4 * k + mat + 1))
            nc.scalar.activation(m.qk[:, buf, slot, 0, :], m.acc[:, mat, :], ACT.Identity,
                                 bias=act_bias(m.params, name, k % PAIRS)).then_inc(s.qk_hi, 1)

    hi(0, 0)

    def step(i, k, more):
        if more:
            hi(*following(i, k, 8))
        if k % PAIRS == PAIRS - 1:
            t = i * 2 + k // PAIRS
            act.wait_ge(s.mag2_done, t + 1)
            nc.scalar.activation(m.mag[:, :], m.mag2[:, :], ACT.Sqrt).then_inc(s.mag_done, 1)
            act.wait_ge(s.shifted, t + 1)
            nc.scalar.activation(m.mag2[:, :], m.mag[:, :], ACT.Exp, scale=HD ** -0.5).then_inc(s.exp_done, 1)

    rolled(act, STEPS_Q // 8, 8, step, 1)


def qk_vector(nc, dve, io, m, s):
    dve.wait_ge(s.block_done, HALVES * PER_HALF)
    dve.wait_ge(s.stored, 32 * 32 * HALVES)
    dve.wait_ge(s.late_loaded, 16 * LATE_DMAS)

    def lo(i, k):
        buf = k % QK_BUFS
        for mat, slot, name in MATRICES:
            dve.wait_ge(s.qk_hi, i * 32 + (4 * k + mat + 1))
            nc.vector.scalar_tensor_tensor(out=m.qk[:, buf, slot, 1, :], in0=m.acc[:, mat, :],
                                           scalar=act_bias(m.params, name, k % PAIRS),
                                           in1=m.qk[:, buf, slot, 0, :].bitcast(F32),
                                           op0=ALU.add, op1=ALU.subtract).then_inc(s.qk_lo, 1)
        dve.wait_ge(s.qk_lo, i * 32 + (4 * k + 4))
        nc.vector.tensor_scalar(m.qk[:, buf, NKI, :, :], m.qk[:, buf, KI, :, :].bitcast(F32), -1.0, None,
                                ALU.mult).then_inc(s.nki_done, 1)

    def take_scores(i, k):
        j = k % PAIRS
        for bank in range(4):
            dve.wait_ge(s.scored, i * 32 + (4 * k + bank + 1))
            if from_step(i, k, 1):
                dve.wait_ge(s.compacted, i * 32 + (4 * k + bank - 3))
            nc.vector.tensor_tensor(m.masked[:, bank, :].rearrange("p (a r) -> p a r", r=32),
                                    m.stat[:, bank, :].rearrange("p (a r) -> p a r", r=32),
                                    m.own_row[:, None, :].to_broadcast([P, 16, 32]), ALU.mult).then_inc(s.masked, 1)
        for bank in range(4):
            gp, hh = bank // 2, bank % 2
            dve.wait_ge(s.masked, i * 32 + (4 * k + bank + 1))
            nc.vector.tensor_reduce(m.compact[:, j, hh, gp, :], m.masked[:, bank, :].rearrange("p (a r) -> p a r", r=32),
                                    AX.X, ALU.add).then_inc(s.compacted, 1)

    def softmax(i, k):
        t = i * 2 + k // PAIRS
        flat = m.compact.rearrange("p j h g w -> p (j h g w)")
        dve.wait_ge(s.compacted, t * 16 + 16)
        nc.vector.tensor_tensor(m.squares[:, :], flat, flat, ALU.mult).then_inc(s.sq_done, 1)
        dve.wait_ge(s.sq_done, t + 1)
        sq = m.squares[:, :].rearrange("p (a k m) -> p a k m", k=2, m=N)
        mag2, mag = (x[:, :].rearrange("p (a m) -> p a m", m=N) for x in (m.mag2, m.mag))
        nc.vector.scalar_tensor_tensor(out=mag2, in0=sq[:, :, 0, :], scalar=1e-8, in1=sq[:, :, 1, :],
                                       op0=ALU.add, op1=ALU.add).then_inc(s.mag2_done, 1)
        dve.wait_ge(s.mag_done, t + 1)
        nc.vector.tensor_reduce(m.top[:, :], mag, AX.X, ALU.max).then_inc(s.max_done, 1)
        dve.wait_ge(s.max_done, t + 1)
        nc.vector.tensor_tensor(mag, mag, m.top[:, :, None].to_broadcast([P, 32, N]), ALU.subtract).then_inc(s.shifted, 1)
        dve.wait_ge(s.exp_done, t + 1)
        nc.vector.tensor_reduce(m.total[:, :], mag2, AX.X, ALU.add).then_inc(s.total_done, 1)
        dve.wait_ge(s.total_done, t + 1)
        nc.vector.reciprocal(m.inverse[:, :], m.total[:, :]).then_inc(s.inverse_done, 1)
        dve.wait_ge(s.inverse_done, t + 1)
        nc.vector.tensor_tensor(m.weights[:, bass.ts(t, P)].rearrange("p (a m) -> p a m", m=N), mag2,
                                m.inverse[:, :, None].to_broadcast([P, 32, N]), ALU.mult).then_inc(s.softmaxed, 1)

    lo(0, 0)

    def step(i, k, more):
        if more:
            lo(*following(i, k, 8))
        take_scores(i, k)
        if k % PAIRS == PAIRS - 1:
            softmax(i, k)

    rolled(dve, STEPS_Q // 8, 8, step, 1)



LATE_PAIR = X_UNITS // 2 + HALVES * (PER_HALF + X_UNITS // 2)


def matrix_slot(m, mat, k):
    return [m.x[:, part, bass.ts(2 * mat + k, UNIT)] for part in range(2)]


def matrix(m, mat, c, cols):
    return [m.x[:, part, mat * C * D + c * D:mat * C * D + (c + 1) * D][:, cols] for part in range(2)]


def load_matrix(sp, io, m, s, index):
    q = LATE_PAIR + index
    for k in range(2):
        sp.wait_ge(s.lo_done, q * 2 + (k - 1))
        sp.dma_start(m.raw[:, k, :], io.late_units[index * 2 + k]).then_inc(s.raw_loaded[k], 16)


def values_sync(nc, sp, io, m, s):
    for index in range(4):
        load_matrix(sp, io, m, s, index)
        if index == 0:
            sp.wait_ge(s.projected, 4 * STEPS_Q)
            load_tile(sp, m, io.s_scr, 0, 0, s.v_tile_loaded)
    with sp.Fori(1, TILES) as t:
        sp.wait_ge(s.gathered, t * 4)
        load_tile(sp, m, io.s_scr, 0, t, s.v_tile_loaded)


def values_tensor(nc, pe, io, m, s):
    grouped = m.h[:, 1, :].rearrange("p (g a b c w) -> p g a b c w", g=GROUPS, a=2, b=2, c=C)

    def value(t, g):
        pe.wait_ge(s.gathered, t * 4 + (g + 1))
        for ri in range(2):
            if g or not isinstance(t, int) or t:
                pe.wait_ge(s.v_lo, t * 8 + (2 * g + ri - 1))
            for c in range(C):
                st = [grouped[:, g, ri, part, c, :] for part in range(2)]
                last = product(nc, m.stat[:, ri, :], st, matrix(m, ri, c, slice(0, D)), c == 0, c == C - 1)
            last.then_inc(s.v_done, 1)

    def turn(t):
        pe.wait_ge(s.spread_done, t + 1)
        if not isinstance(t, int) or t:
            pe.wait_ge(s.at_lo, t * 8 - 8)
        for a in range(N):
            last = nc.tensor.matmul(m.stat[:, 2, 0:P], m.select[:, a, :], m.spread[:, a, :],
                                    start=a == 0, stop=a == N - 1)
        last.then_inc(s.wt_done, 1)

    def weigh(t, g):
        pe.wait_ge(s.v_lo, t * 8 + (2 * g + 2))
        pe.wait_ge(s.wf_hi, t * 4 + (g + 1))
        pe.wait_ge(s.wf_lo, t * 4 + (g + 1))
        if g or not isinstance(t, int) or t:
            pe.wait_ge(s.ot_lo, t * 16 + 4 * g)
        for ri in range(2):
            for j in range(PAIRS):
                st = [m.v[:, g % 2, ri, part, bass.ts(j, P)] for part in range(2)]
                mv = [m.wf[:, part, bass.ts(j, 2 * P)] for part in range(2)]
                last = product(nc, m.acc[:, 2 * ri + j // 2, bass.ts(j % 2, 2 * P)], st, mv, True, True)
            last.then_inc(s.weighed, 1)

    def project(t, more):
        pe.wait_ge(s.ot_lo, t * 16 + 16)
        if more:
            pe.wait_ge(s.wt_lo, t + 2)
        for e in range(2 * C):
            ri, ec = divmod(e, C)
            if e or not isinstance(t, int) or t:
                if e >= 2 or not isinstance(t, int) or t:
                    pe.wait_ge(s.at_lo, t * 8 + (e - 1))
            for j in range(PAIRS):
                last = product(nc, m.stat[:, 2 + e % 2, :], matrix(m, 2 + ri, j, bass.ts(ec, P)),
                               [m.ot[:, ri, part, j, :] for part in range(2)], j == 0, j == PAIRS - 1)
            last.then_inc(s.attn_done, 1)

    pe.wait_ge(s.lo_done, 2 * (LATE_PAIR + 2))
    pe.wait_ge(s.compacted, 4 * STEPS_Q)
    value(0, 0)
    turn(0)
    pe.wait_ge(s.lo_done, 2 * (LATE_PAIR + 4))
    pe.wait_ge(s.bv_done, 2)
    for e in range(2 * C):
        ri, ec = divmod(e, C)
        for j in range(PAIRS):
            for part in range(2):
                last = nc.tensor.matmul(m.stat[:, 3, 2 * e:2 * e + 2], matrix(m, 2 + ri, j, bass.ts(ec, P))[part],
                                        m.bv[:, ri, j, :], start=j == 0 and part == 0, stop=j == PAIRS - 1 and part == 1)
    last.then_inc(s.bias_done, 1)

    def tile(t, _, more):
        for g in range(GROUPS):
            if g + 1 < GROUPS:
                value(t, g + 1)
            elif more:
                value(t + 1, 0)
                turn(t + 1)
            weigh(t, g)
        project(t, more)

    rolled(pe, TILES, 1, tile, 1)


def values_scalar(nc, act, io, m, s):
    act.wait_ge(s.projected, 4 * STEPS_Q)
    def v_hi(t, g):
        if g >= 2 or not isinstance(t, int) or t:
            act.wait_ge(s.weighed, t * 8 + (2 * g - 2))
        for ri in range(2):
            act.wait_ge(s.v_done, t * 8 + (2 * g + ri + 1))
            nc.scalar.copy(m.v[:, g % 2, ri, 0, :], m.stat[:, ri, :]).then_inc(s.v_hi, 1)

    def wt_hi(t):
        act.wait_ge(s.wt_done, t + 1)
        if not isinstance(t, int) or t:
            act.wait_ge(s.wf_hi, t * 4)
            act.wait_ge(s.wf_lo, t * 4)
        nc.scalar.copy(m.wt[:, 0, :], m.stat[:, 2, 0:P]).then_inc(s.wt_hi, 1)

    def ot_hi(t, g):
        if g == 0 and (not isinstance(t, int) or t):
            act.wait_ge(s.attn_done, t * 8)
        for ri in range(2):
            act.wait_ge(s.weighed, t * 8 + (2 * g + ri + 1))
            for hh in range(2):
                out, src = head_blocks(m, ri, hh, g)
                nc.scalar.copy(out[0], src).then_inc(s.ot_hi, 1)

    def at_hi(t):
        for e in range(2 * C):
            act.wait_ge(s.attn_done, t * 8 + (e + 1))
            if e >= 2 or not isinstance(t, int) or t:
                act.wait_ge(s.at_stored[e % 2], t * 128 + 32 * (e // 2))
            nc.scalar.activation(stage(m, e)[0].bitcast(F32R), m.stat[:, 2 + e % 2, :], ACT.Identity,
                                 bias=m.bo[:, e:e + 1]).then_inc(s.at_hi, 1)

    for mat in range(4):
        for k in range(2):
            cut_hi(nc, act, m, s, LATE_PAIR + mat, matrix_slot(m, mat, k), k)
        if mat == 0:
            act.wait_ge(s.scored, 4 * STEPS_Q)
            act.wait_ge(s.softmaxed, TILES)
            at = PARAM["v_r"]
            nc.scalar.copy(m.bv[:, :, :, 0].rearrange("p a b -> p (a b)"), m.params[:, at:at + 8]).then_inc(s.bv_done, 1)
        if mat == 1:
            v_hi(0, 0)
    wt_hi(0)
    act.wait_ge(s.bo_done, 2)

    def tile(t, _, more):
        for g in range(GROUPS):
            if g + 1 < GROUPS:
                v_hi(t, g + 1)
            elif more:
                v_hi(t + 1, 0)
                wt_hi(t + 1)
            ot_hi(t, g)
        at_hi(t)

    rolled(act, TILES, 1, tile, 1)


def head_blocks(m, ri, hh, g):
    part = slice(64 * hh, 64 * hh + 64)
    out = [m.ot[part, ri, half, :, :].rearrange("p j (n r) -> p j n r", n=N)[:, :, :, 32 * g:32 * g + 32] for half in range(2)]
    src = m.acc[part, 2 * ri:2 * ri + 2, :].rearrange("p b (j h n r) -> p (b j) h n r", j=2, h=2, n=N)[:, :, hh, :, :]
    return out, src


def stage(m, e):
    return m.raw[:, e % 2, 0:512], m.raw[:, e % 2, 512:1024]


def values_vector(nc, dve, io, m, s):
    tiles = m.h[:, 0, :].rearrange("p (q g r) -> p q g r", g=GROUPS, r=32)
    grouped = m.h[:, 1, :].rearrange("p (g q r) -> p g q r", g=GROUPS, r=32)

    def gather(t, g):
        dve.wait_ge(s.v_tile_loaded, t * (16 * TILE_DMAS) + 16 * TILE_DMAS)
        if not isinstance(t, int) or t:
            dve.wait_ge(s.v_done, t * 8 + (2 * g - 6))
        nc.vector.tensor_copy(grouped[:, g], tiles[:, :, g, :].bitcast(F32)).then_inc(s.gathered, 1)

    def spread(t):
        if not isinstance(t, int) or t:
            dve.wait_ge(s.wt_done, t)
        w = m.weights[:, bass.ts(t, P)].rearrange("p (h m) -> p m h", m=N)
        nc.vector.tensor_tensor(m.spread[:, :, :].rearrange("p m (h n) -> p m h n", n=N),
                                w[:, :, :, None].to_broadcast([P, N, 32, N]),
                                m.own_n[:, None, None, :].to_broadcast([P, N, 32, N]), ALU.mult).then_inc(s.spread_done, 1)

    def v_lo(t, g):
        for ri in range(2):
            dve.wait_ge(s.v_hi, t * 8 + (2 * g + ri + 1))
            nc.vector.tensor_tensor(m.v[:, g % 2, ri, 1, :], m.stat[:, ri, :], m.v[:, g % 2, ri, 0, :].bitcast(F32),
                                    ALU.subtract).then_inc(s.v_lo, 1)

    def wt_lo(t):
        dve.wait_ge(s.wt_hi, t + 1)
        nc.vector.tensor_tensor(m.wt[:, 1, :], m.stat[:, 2, 0:P], m.wt[:, 0, :].bitcast(F32), ALU.subtract).then_inc(s.wt_lo, 1)

    def ot_lo(t, g):
        for ri in range(2):
            for hh in range(2):
                out, src = head_blocks(m, ri, hh, g)
                dve.wait_ge(s.ot_hi, t * 16 + (4 * g + 2 * ri + hh + 1))
                nc.vector.tensor_tensor(out[1], src, out[0].bitcast(F32), ALU.subtract).then_inc(s.ot_lo, 1)

    def at_lo(t):
        for e in range(2 * C):
            dve.wait_ge(s.at_hi, t * 8 + (e + 1))
            nc.vector.scalar_tensor_tensor(out=stage(m, e)[1].bitcast(F32R), in0=m.stat[:, 2 + e % 2, :],
                                           scalar=m.bo[:, e:e + 1], in1=stage(m, e)[0],
                                           op0=ALU.add, op1=ALU.subtract).then_inc(s.at_lo, 1)

    for mat in range(4):
        for k in range(2):
            cut_lo(nc, dve, m, s, LATE_PAIR + mat, matrix_slot(m, mat, k), k)
        if mat == 0:
            dve.wait_ge(s.scored, 4 * STEPS_Q)
            dve.wait_ge(s.bv_done, 1)
            at = PARAM["v_r"]
            nc.vector.tensor_tensor(m.bv[:, :, :, 1].rearrange("p a b -> p (a b)"), m.params[:, at:at + 8],
                                    m.bv[:, :, :, 0].rearrange("p a b -> p (a b)").bitcast(F32), ALU.subtract).then_inc(s.bv_done, 1)
            for g in range(GROUPS):
                gather(0, g)
            dve.wait_ge(s.softmaxed, TILES)
            spread(0)
        if mat == 1:
            v_lo(0, 0)
    wt_lo(0)
    expand(nc, nc.vector, dve, m, s, 0, 0, 0)
    dve.wait_ge(s.bias_done, 1)
    nc.vector.tensor_reduce(m.bo[:, :], m.stat[:, 3, 0:16].rearrange("p (e k) -> p e k", k=2), AX.X, ALU.add).then_inc(s.bo_done, 1)
    dve.wait_ge(s.bo_done, 1)
    at = PARAM["o_r"]
    nc.vector.tensor_tensor(m.bo[:, :], m.bo[:, :], m.params[:, at:at + 8], ALU.add).then_inc(s.bo_done, 1)

    def tile(t, _, more):
        for g in range(GROUPS):
            if g + 1 < GROUPS:
                v_lo(t, g + 1)
            elif more:
                v_lo(t + 1, 0)
            if g == 1 and more:
                spread(t + 1)
            if g >= 2 and more:
                for other in (2 * g - 4, 2 * g - 3):
                    gather(t + 1, other)
            if g == 3 and more:
                wt_lo(t + 1)
            ot_lo(t, g)
            if g + 1 < GROUPS:
                expand(nc, nc.vector, dve, m, s, t, g + 1, 0)
            elif more:
                expand(nc, nc.vector, dve, m, s, t + 1, 0, 0)
        at_lo(t)

    rolled(dve, TILES, 1, tile, 1)


def expand(nc, engine, queue, m, s, t, g, part):
    queue.wait_ge(s.wt_lo if part else s.wt_hi, t + 1)
    if g or not isinstance(t, int) or t:
        queue.wait_ge(s.weighed, t * 8 + 2 * g)
    w = m.wt[:, part, :].bitcast(F32).rearrange("p (h g n) -> p h g n", g=GROUPS, n=N)[:, :, g, :]
    engine.tensor_tensor(m.wf[:, part, :].rearrange("p (h n r) -> p h n r", n=N, r=32),
                         w[:, :, :, None].to_broadcast([P, HEADS, N, 32]),
                         m.own_row[:, None, None, :].to_broadcast([P, HEADS, N, 32]),
                         ALU.mult).then_inc(s.wf_lo if part else s.wf_hi, 1)


def values_pool(nc, pool, io, m, s):
    pool.wait_ge(s.scored, 4 * STEPS_Q)
    pool.wait_ge(s.softmaxed, TILES)

    def tile(t, _, more):
        for g in range(GROUPS):
            expand(nc, nc.gpsimd, pool, m, s, t, g, 1)
        for e in range(2 * C):
            ri, ec = divmod(e, C)
            pool.wait_ge(s.at_lo, t * 8 + (e + 1))
            for part in range(2):
                pool.dma_start(io.a_scr[ri, part, :, ec, :, bass.ts(t, P)].rearrange("n p r -> p n r"),
                               stage(m, e)[part].rearrange("p (n r) -> p n r", n=N)).then_inc(s.at_stored[e % 2], 16)

    rolled(pool, TILES, 1, tile)



ROWS = 4
I_STEPS = HALVES * N
I_TILES = I_STEPS * ROWS
PAIRS_OF_N = [(0, 1), (0, 2), (0, 3), (1, 2), (1, 3), (2, 3)]
TINY = 2.0 ** -100
M_FIRST = 4 + 2 * N
LATE_ORDER = list(range(4)) + list(range(4, 4 + 2 * N)) * HALVES + [M_FIRST + k for k in range(5)]


def bank(m, b):
    return m.acc[:, b, :] if b < 4 else m.stat[:, b - 4, :]


def quarter(m, q):
    return m.h[:, 0, q * 4096:(q + 1) * 4096].rearrange("p (a b c r) -> p a b c r", a=2, b=2, c=C)


def sup_view(m):
    return m.h[:, 1, :].rearrange("p (b a c r) -> p b a c r", a=2, b=2, c=C)


def load_stream(sp, io, m, s, at, units=2):
    for k in range(units):
        sp.wait_ge(s.lo_done, (LATE_PAIR + at) * 2 + k - 1)
        sp.dma_start(m.raw[:, k, :], io.late_units[LATE_ORDER[at] * 2 + k]).then_inc(s.raw_loaded[k], 16)


def final_sync(nc, sp, io, m, s):
    def load_quarter(step, q):
        half, n = divmod(step, N)
        a = step * 2 + q
        if a >= 2:
            sp.wait_ge(s.i_done, 2 * (a - 1))
        rows = half * HALF + q * 256
        for ri in range(2):
            for part in range(2):
                sp.dma_start(quarter(m, q)[:, ri, part].bitcast(F32),
                             io.a_scr[ri, part, n, :, :, rows:rows + 256].rearrange("c p r -> p c r")
                             ).then_inc(s.quarter_loaded[q], 16)

    for e in range(2):
        sp.wait_ge(s.at_stored[e], 128 * TILES)
    for mat in range(2):
        load_stream(sp, io, m, s, 4 + mat)
    for q in range(2):
        load_quarter(0, q)
    for mat in range(2):
        load_stream(sp, io, m, s, 6 + mat)
    for step in range(1, I_STEPS):
        for q in range(2):
            load_quarter(step, q)
        for mat in range(2):
            load_stream(sp, io, m, s, 6 + 2 * step + mat)
    for mat in range(2):
        load_stream(sp, io, m, s, 22 + mat)
    load_stream(sp, io, m, s, 24, 1)


def final_tensor(nc, pe, io, m, s):
    def interfere(step):
        pe.wait_ge(s.lo_done, (LATE_PAIR + 6 + 2 * step) * 2)
        for q in range(2):
            pe.wait_ge(s.quarter_loaded[q], 64 * (step + 1))
            for tk in range(2):
                k = (step * 2 + q) * 2 + tk
                if k >= 2:
                    pe.wait_ge(s.r_done, k - 1)
                    pe.wait_ge(s.i_out, k - 1)
                for out, parts in enumerate((((0, 0),), ((1, 1),), ((0, 1), (1, 0)))):
                    for x, (ri, mat) in enumerate(parts):
                        for c in range(C):
                            st = [quarter(m, q)[:, ri, part, c, bass.ts(tk, P)] for part in range(2)]
                            last = product(nc, bank(m, 3 * (k % 2) + out), st,
                                           matrix(m, 2 * (step % 2) + mat, c, slice(0, D)),
                                           x == 0 and c == 0, x == len(parts) - 1 and c == C - 1)
                last.then_inc(s.i_done, 1)
                if step > N and k % 4 == 0:
                    turn(step - N - 1)

    def turn(x):
        pe.wait_ge(s.sup_done, x + 1)
        if x:
            pe.wait_ge(s.sup_lo, 2 * x)
        for ri in range(2):
            for c in range(C):
                last = nc.tensor.transpose(bank(m, 6 + ri)[:, bass.ts(c, P)], m.u[:, ri * D + c * P:ri * D + (c + 1) * P],
                                           m.table[:, :])
            last.then_inc(s.turned, 1)

    def measure(h):
        pe.wait_ge(s.sup_lo, 8 * (h + 1))
        if h:
            pe.wait_ge(s.y_out, h)
        for e in range(C):
            u = h * C + e
            if e >= 2:
                pe.wait_ge(s.mr_done, u - 1)
                pe.wait_ge(s.mi_sq, u - 1)
            for out, parts in enumerate((((0, 0),), ((1, 1),), ((1, 0), (0, 1)))):
                for x, (mat, ri) in enumerate(parts):
                    for c in range(C):
                        mv = [sup_view(m)[:, part, ri, c, :] for part in range(2)]
                        last = product(nc, bank(m, 3 * (e % 2) + out), matrix(m, mat, c, bass.ts(e, P)), mv,
                                       x == 0 and c == 0, x == len(parts) - 1 and c == C - 1)
            last.then_inc(s.measured, 1)

    def post(h):
        pe.wait_ge(s.amp_lo, C * (h + 1))
        for e in range(C):
            u = h * C + e
            if e >= 2:
                pe.wait_ge(s.z_sq, u - 1)
            for c in range(C):
                mv = [m.a[:, part, bass.ts(c, HALF)] for part in range(2)]
                last = product(nc, bank(m, e % 2), matrix(m, 2, c, bass.ts(e, P)), mv, c == 0, c == C - 1)
            last.then_inc(s.posted, 1)
        pe.wait_ge(s.z_sums, 2 * (h + 1))
        for k in range(2):
            last = nc.tensor.matmul(bank(m, 4 + k), m.mean_of_out[:, :], m.pair[:, k, :], start=True, stop=True)
        last.then_inc(s.z_means, 1)

    def top(h):
        pe.wait_ge(s.z_lo, C * (h + 1))
        for j in range(C + 1):
            u = h * C + j
            if j < C:
                if j >= 2:
                    pe.wait_ge(s.top_sum, u - 1)
                for c in range(C):
                    mv = [m.a[:, part, bass.ts(c, HALF)] for part in range(2)]
                    last = product(nc, bank(m, j % 2), matrix(m, 3, c, bass.ts(j, P)), mv, c == 0, c == C - 1)
                last.then_inc(s.topped, 1)
            if j:
                pe.wait_ge(s.h1_lo, u)
                for k in range(2):
                    st = [m.top2[:, part, (j - 1) * 256 + k * P:(j - 1) * 256 + (k + 1) * P] for part in range(2)]
                    mv = [m.h1[:, (j - 1) % 2, part, :] for part in range(2)]
                    last = product(nc, bank(m, 2 + k), st, mv, j == 1, j == C)
                last.then_inc(s.h2_part, 1)
        pe.wait_ge(s.h2_done, 2 * (h + 1))
        for k in range(2):
            last = nc.tensor.matmul(bank(m, 4)[0:1, :], act_bias(m.params, "w3", k), m.pair[:, k, :],
                                    start=k == 0, stop=k == 1)
        last.then_inc(s.y_done, 1)

    pe.wait_ge(s.at_lo, 2 * C * TILES)
    for step in range(I_STEPS):
        interfere(step)
    turn(3)
    pe.wait_ge(s.lo_done, (LATE_PAIR + 24) * 2 + 1)
    pe.wait_ge(s.mean_loaded, 16)
    for x, part in ((4, measure), (5, post), (6, top)):
        part(0)
        turn(x)
    turn(7)
    for part in (measure, post, top):
        part(1)


def final_scalar(nc, act, io, m, s):
    def cut(at, mat, units=2):
        for k in range(units):
            dst = matrix_slot(m, mat, k) if mat < 4 else [m.top2[:, part, :] for part in range(2)]
            cut_hi(nc, act, m, s, LATE_PAIR + at, dst, k)

    def take(step, k4):
        k = step * 4 + k4
        b = 3 * (k % 2)
        act.wait_ge(s.i_done, k + 1)
        if k:
            act.wait_ge(s.r_done, k)
        nc.scalar.copy(m.aiwi[:, :], bank(m, b + 1)).then_inc(s.aiwi_out, 1)
        if k >= 2:
            act.wait_ge(s.ri_stored[k % 2], 16 * (k // 2))
        nc.scalar.copy(m.stage[:, k % 2, 512:1024], bank(m, b + 2)).then_inc(s.i_out, 1)

    def squares(x):
        act.wait_ge(s.ri_loaded, 16 * (x + 1))
        if x:
            act.wait_ge(s.f_done, 12 * x)
        nc.scalar.activation(m.sq[:, :], m.ri[:, :], ACT.Square).then_inc(s.x_sq, 1)
        act.wait_ge(s.x_clamped, x + 1)
        nc.scalar.activation(m.n2[:, :], m.n2[:, :], ACT.Sqrt).then_inc(s.x_root, 1)

    def norm(x):
        act.wait_ge(s.sup_sum, x + 1)
        nc.scalar.activation(m.sq[:, 0:1024], m.u[:, 0:1024], ACT.Square, accum_out=m.norms[:, 0:1]).then_inc(s.norm_sum, 1)
        act.wait_ge(s.norm_eps, x + 1)
        nc.scalar.activation(m.norms[:, 2:3], m.norms[:, 1:2], ACT.Sqrt).then_inc(s.norm_root, 1)

    def sup_hi(x):
        h, r = divmod(x, ROWS)
        if h and r == 0:
            act.wait_ge(s.measured, C)
        for ri in range(2):
            act.wait_ge(s.turned, 2 * x + ri + 1)
            nc.scalar.copy(sup_view(m)[:, 0, ri, :, bass.ts(r, P)],
                           bank(m, 6 + ri).rearrange("p (c r) -> p c r", r=P)).then_inc(s.sup_hi, 1)

    def measure(h):
        for e in range(C):
            u = h * C + e
            act.wait_ge(s.measured, u + 1)
            if u % C == 0 and h:
                act.wait_ge(s.y_done, h)
            nc.scalar.copy(m.pair[:, 0, :], bank(m, 3 * (e % 2) + 1)).then_inc(s.misi_out, 1)
            nc.scalar.activation(m.pair[:, 1, :], bank(m, 3 * (e % 2) + 2), ACT.Square).then_inc(s.mi_sq, 1)
            act.wait_ge(s.amp_sq, u + 1)
            nc.scalar.activation(m.pair[:, 0, :], m.pair[:, 0, :], ACT.Sqrt).then_inc(s.amp_root, 1)
            act.wait_ge(s.amp_root, u + 1)
            nc.scalar.copy(m.a[:, 0, bass.ts(e, HALF)], m.pair[:, 0, :]).then_inc(s.amp_hi, 1)
            act.wait_ge(s.amp_lo, u + 1)

    def post(h):
        z = m.raw.rearrange("p a w -> p (a w)")
        act.wait_ge(s.lo_done, (LATE_PAIR + 24) * 2 + 1)
        if h:
            act.wait_ge(s.z_lo, C * h)
        for e in range(C):
            u = h * C + e
            cols = bass.ts(e, HALF)
            act.wait_ge(s.posted, u + 1)
            if e:
                act.wait_ge(s.z_sq_added, u)
            bias = act_bias(m.params, "post_b", e)
            nc.scalar.activation(z[:, cols], bank(m, e % 2), ACT.Identity, bias=bias).then_inc(s.z_pre, 1)
            nc.scalar.activation(m.pair[:, 0, :], bank(m, e % 2), ACT.Square, bias=bias).then_inc(s.z_sq, 1)
        act.wait_ge(s.z_means, h + 1)
        nc.scalar.activation(m.pair[:, 0, :], bank(m, 4), ACT.Square).then_inc(s.z_mean_sq, 1)
        act.wait_ge(s.z_var, h + 1)
        nc.scalar.activation(m.pair[:, 0, :], m.pair[:, 1, :], ACT.Sqrt).then_inc(s.z_std, 1)
        for e in range(C):
            u = h * C + e
            cols = bass.ts(e, HALF)
            act.wait_ge(s.z_scaled, u + 1)
            nc.scalar.activation(z[:, cols], z[:, cols], ACT.Gelu, bias=act_bias(m.params, "post_be", e),
                                 scale=act_bias(m.params, "post_g", e)).then_inc(s.z_gelu, 1)
            act.wait_ge(s.z_gelu, u + 1)
            nc.scalar.copy(m.a[:, 0, cols], z[:, cols]).then_inc(s.z_hi, 1)

    def top(h):
        for j in range(C):
            u = h * C + j
            act.wait_ge(s.top_sum, u + 1)
            if u >= 2:
                act.wait_ge(s.h2_part, u - 1)
            nc.scalar.activation(m.h1[:, j % 2, 0, :], m.top_x[:, j % 2, :], ACT.Relu).then_inc(s.h1_hi, 1)
        act.wait_ge(s.h2_part, C * (h + 1))
        for k in range(2):
            nc.scalar.activation(m.pair[:, k, :], bank(m, 2 + k), ACT.Relu,
                                 bias=act_bias(m.params, "top2", k)).then_inc(s.h2_done, 1)
        act.wait_ge(s.y_done, h + 1)
        nc.scalar.copy(m.top_x[0:1, 0, :], bank(m, 4)[0:1, :]).then_inc(s.y_out, 1)
        act.wait_ge(s.y_out, h + 1)
        act.dma_start(io.y[h:h + 1, :], m.top_x[0:1, 0, :]).then_inc(s.y_stored, 16)

    act.wait_ge(s.attn_done, 2 * C * TILES)
    act.wait_ge(s.at_lo, 2 * C * TILES)
    for mat in range(4):
        cut(4 + mat, mat)
    for step in range(I_STEPS):
        if step >= N:
            squares(step - N)
        for k4 in range(4):
            take(step, k4)
            if step > N and k4 == 1:
                sup_hi(step - N - 1)
        if step + 2 < I_STEPS:
            for mat in range(2):
                cut(8 + 2 * step + mat, 2 * (step % 2) + mat)
        if step == I_STEPS - 2:
            for mat in range(2):
                cut(20 + mat, mat)
        if step >= N:
            norm(step - N)
    for mat in range(2):
        cut(22 + mat, 2 + mat)
    act.wait_ge(s.ri_stored[0], 16 * I_TILES // 2)
    act.wait_ge(s.ri_stored[1], 16 * I_TILES // 2)
    act.wait_ge(s.r_done, I_TILES)
    cut(24, 4, 1)
    for x, part in ((4, measure), (5, post), (6, top)):
        sup_hi(x - 1)
        squares(x)
        norm(x)
        part(0)
    squares(7)
    sup_hi(6)
    norm(7)
    sup_hi(7)
    for part in (measure, post, top):
        part(1)
    act.wait_ge(s.y_stored, 32)


def final_vector(nc, dve, io, m, s):
    def cut(at, mat, units=2):
        for k in range(units):
            dst = matrix_slot(m, mat, k) if mat < 4 else [m.top2[:, part, :] for part in range(2)]
            cut_lo(nc, dve, m, s, LATE_PAIR + at, dst, k)

    def take(step, k4):
        k = step * 4 + k4
        dve.wait_ge(s.aiwi_out, k + 1)
        if k >= 2:
            dve.wait_ge(s.ri_stored[k % 2], 16 * (k // 2))
        nc.vector.tensor_tensor(m.stage[:, k % 2, 0:512], bank(m, 3 * (k % 2)), m.aiwi[:, :], ALU.subtract).then_inc(s.r_done, 1)

    ri = m.ri[:, :].rearrange("p (n k d) -> p n k d", n=N, k=2)
    u = m.u[:, :].rearrange("p (n k d) -> p n k d", n=N, k=2)
    sq = m.sq[:, :].rearrange("p (n k d) -> p n k d", n=N, k=2)
    n2 = m.n2[:, :].rearrange("p (n d) -> p n d", n=N)

    def directions(x):
        dve.wait_ge(s.x_sq, x + 1)
        nc.vector.tensor_tensor(n2, sq[:, :, 0, :], sq[:, :, 1, :], ALU.add).then_inc(s.x_sum, 1)
        dve.wait_ge(s.x_sum, x + 1)
        if x:
            dve.wait_ge(s.zero_pairs, 6 * x)
        nc.vector.tensor_scalar(m.zero[:, :], m.n2[:, :], 0.0, None, ALU.is_equal).then_inc(s.x_zero, 1)
        nc.vector.tensor_scalar(m.n2[:, :], m.n2[:, :], TINY, None, ALU.max).then_inc(s.x_clamped, 1)

    def cosines(x):
        dve.wait_ge(s.x_root, x + 1)
        nc.vector.reciprocal(m.n2[:, :], m.n2[:, :]).then_inc(s.x_inverse, 1)
        dve.wait_ge(s.x_inverse, x + 1)
        if x:
            dve.wait_ge(s.turned, 2 * x)
        nc.vector.tensor_tensor(u, ri, n2[:, :, None, :].to_broadcast([P, N, 2, D]), ALU.mult).then_inc(s.u_done, 1)
        dve.wait_ge(s.u_done, x + 1)
        for n, (i, j) in enumerate(PAIRS_OF_N[:4]):
            nc.vector.tensor_tensor(sq[:, n], u[:, i], u[:, j], ALU.mult).then_inc(s.pair_mul, 1)
        dve.wait_ge(s.pair_mul, 6 * x + 4)
        nc.vector.tensor_tensor(sq[:, :, 0, :], sq[:, :, 0, :], sq[:, :, 1, :], ALU.add).then_inc(s.pair_sum, 1)
        dve.wait_ge(s.pair_sum, 3 * x + 1)
        for n, (i, j) in enumerate(PAIRS_OF_N[4:]):
            nc.vector.tensor_tensor(sq[:, 2 * n:2 * n + 2, 1, :], u[:, i], u[:, j], ALU.mult).then_inc(s.pair_mul, 1)
        for n in range(2):
            dve.wait_ge(s.pair_mul, 6 * x + 5 + n)
            nc.vector.tensor_tensor(sq[:, 2 * n, 1, :], sq[:, 2 * n, 1, :], sq[:, 2 * n + 1, 1, :], ALU.add).then_inc(s.pair_sum, 1)
        dve.wait_ge(s.zero_pairs, 6 * x + 6)
        dve.wait_ge(s.pair_sum, 3 * x + 3)
        zp = m.n2[:, 0:1536].bitcast(BF16).rearrange("p (a d) -> p a d", d=D)
        nc.vector.tensor_tensor(sq[:, :, 0, :], sq[:, :, 0, :], zp[:, 0:4, :], ALU.add).then_inc(s.cos_done, 1)
        nc.vector.tensor_tensor(sq[:, 0:4:2, 1, :], sq[:, 0:4:2, 1, :], zp[:, 4:6, :], ALU.add).then_inc(s.cos_done, 1)
        dve.wait_ge(s.cos_done, 2 * x + 2)

    def cosine(i, j):
        n = PAIRS_OF_N.index((min(i, j), max(i, j)))
        return sq[:, n, 0, :] if n < 4 else sq[:, 2 * (n - 4), 1, :]

    def superpose(x):
        def strength(i, j):
            return m.strength[:, x, 4 * i + j:4 * i + j + 1]

        for n in range(3):
            for j in range(N):
                i = [k for k in range(N) if k != j][n]
                if n == 0:
                    ins = nc.vector.tensor_scalar(n2[:, j], cosine(i, j), strength(i, j), strength(j, j), ALU.mult, ALU.add)
                else:
                    dve.wait_ge(s.f_done, 12 * x + 4 * (n - 1) + j + 1)
                    ins = nc.vector.scalar_tensor_tensor(out=n2[:, j], in0=cosine(i, j), scalar=strength(i, j), in1=n2[:, j],
                                                         op0=ALU.mult, op1=ALU.add)
                ins.then_inc(s.f_done, 1)
        dve.wait_ge(s.f_done, 12 * x + 12)
        nc.vector.tensor_tensor(u, ri, n2[:, :, None, :].to_broadcast([P, N, 2, D]), ALU.mult).then_inc(s.fz_done, 1)
        dve.wait_ge(s.fz_done, x + 1)
        nc.vector.tensor_tensor(m.u[:, 0:2048], m.u[:, 0:2048], m.u[:, 2048:4096], ALU.add).then_inc(s.half_sum, 1)
        dve.wait_ge(s.half_sum, x + 1)
        nc.vector.tensor_tensor(m.u[:, 0:1024], m.u[:, 0:1024], m.u[:, 1024:2048], ALU.add).then_inc(s.sup_sum, 1)
        dve.wait_ge(s.norm_sum, x + 1)
        nc.vector.tensor_scalar(m.norms[:, 1:2], m.norms[:, 0:1], 1e-8, None, ALU.add).then_inc(s.norm_eps, 1)
        dve.wait_ge(s.norm_root, x + 1)
        nc.vector.reciprocal(m.norms[:, 3:4], m.norms[:, 2:3]).then_inc(s.norm_inverse, 1)
        dve.wait_ge(s.norm_inverse, x + 1)
        nc.vector.tensor_scalar(m.u[:, 0:1024], m.u[:, 0:1024], m.norms[:, 3:4], None, ALU.mult).then_inc(s.sup_done, 1)

    def sup_lo(x):
        r = x % ROWS
        for k in range(2):
            dve.wait_ge(s.sup_hi, 2 * x + k + 1)
            nc.vector.tensor_tensor(sup_view(m)[:, 1, k, :, bass.ts(r, P)], bank(m, 6 + k).rearrange("p (c r) -> p c r", r=P),
                                    sup_view(m)[:, 0, k, :, bass.ts(r, P)].bitcast(F32), ALU.subtract).then_inc(s.sup_lo, 1)

    def measure(h):
        a, b = m.pair[:, 0, :], m.pair[:, 1, :]
        for e in range(C):
            v = h * C + e
            dve.wait_ge(s.misi_out, v + 1)
            nc.vector.tensor_tensor(a, bank(m, 3 * (e % 2)), a, ALU.subtract).then_inc(s.mr_done, 1)
            dve.wait_ge(s.mr_done, v + 1)
            nc.vector.tensor_tensor(a, a, a, ALU.mult).then_inc(s.mr_sq, 1)
            dve.wait_ge(s.mr_sq, v + 1)
            dve.wait_ge(s.mi_sq, v + 1)
            nc.vector.tensor_tensor(a, a, b, ALU.add).then_inc(s.amp_sq, 1)
            dve.wait_ge(s.amp_hi, v + 1)
            nc.vector.tensor_tensor(m.a[:, 1, bass.ts(e, HALF)], a, m.a[:, 0, bass.ts(e, HALF)].bitcast(F32),
                                    ALU.subtract).then_inc(s.amp_lo, 1)

    def post(h):
        z = m.raw.rearrange("p a w -> p (a w)")
        a, b = m.pair[:, 0, :], m.pair[:, 1, :]
        sums, sums_sq, mean, rstd = (bank(m, k) for k in (2, 3, 4, 5))
        for e in range(C):
            v = h * C + e
            cols = bass.ts(e, HALF)
            dve.wait_ge(s.z_pre, v + 1)
            if e:
                dve.wait_ge(s.z_added, v)
                nc.vector.tensor_tensor(sums, sums, z[:, cols], ALU.add).then_inc(s.z_added, 1)
            else:
                nc.vector.tensor_copy(sums, z[:, cols]).then_inc(s.z_added, 1)
            dve.wait_ge(s.z_sq, v + 1)
            if e:
                dve.wait_ge(s.z_sq_added, v)
                nc.vector.tensor_tensor(sums_sq, sums_sq, a, ALU.add).then_inc(s.z_sq_added, 1)
            else:
                nc.vector.tensor_copy(sums_sq, a).then_inc(s.z_sq_added, 1)
        dve.wait_ge(s.z_added, C * (h + 1))
        dve.wait_ge(s.z_sq_added, C * (h + 1))
        nc.vector.tensor_copy(a, sums).then_inc(s.z_sums, 1)
        nc.vector.tensor_copy(b, sums_sq).then_inc(s.z_sums, 1)
        dve.wait_ge(s.z_mean_sq, h + 1)
        nc.vector.tensor_tensor(b, rstd, a, ALU.subtract).then_inc(s.z_var_raw, 1)
        dve.wait_ge(s.z_var_raw, h + 1)
        nc.vector.tensor_scalar(b, b, 0.0, LN_EPS, ALU.max, ALU.add).then_inc(s.z_var, 1)
        dve.wait_ge(s.z_std, h + 1)
        nc.vector.reciprocal(rstd, a).then_inc(s.z_rstd, 1)
        dve.wait_ge(s.z_rstd, h + 1)
        for e in range(C):
            v = h * C + e
            cols = bass.ts(e, HALF)
            nc.vector.tensor_tensor(z[:, cols], z[:, cols], mean, ALU.subtract).then_inc(s.z_centred, 1)
            dve.wait_ge(s.z_centred, v + 1)
            nc.vector.tensor_tensor(z[:, cols], z[:, cols], rstd, ALU.mult).then_inc(s.z_scaled, 1)
        for e in range(C):
            v = h * C + e
            cols = bass.ts(e, HALF)
            dve.wait_ge(s.z_hi, v + 1)
            nc.vector.tensor_tensor(m.a[:, 1, cols], z[:, cols], m.a[:, 0, cols].bitcast(F32), ALU.subtract).then_inc(s.z_lo, 1)

    def top(h):
        for j in range(C):
            v = h * C + j
            t = m.top_x[:, j % 2, :]
            dve.wait_ge(s.topped, v + 1)
            dve.wait_ge(s.top_x_loaded[j % 2], 16 * (v // 2 + 1))
            nc.vector.tensor_tensor(t, bank(m, j % 2), t, ALU.add).then_inc(s.top_sum, 1)
            dve.wait_ge(s.h1_hi, v + 1)
            dve.wait_ge(s.top_sum, v + 1)
            nc.vector.scalar_tensor_tensor(out=m.h1[:, j % 2, 1, :], in0=t, scalar=0.0, in1=m.h1[:, j % 2, 0, :].bitcast(F32),
                                           op0=ALU.max, op1=ALU.subtract).then_inc(s.h1_lo, 1)

    dve.wait_ge(s.strength_loaded, 16 * TILES * N)
    for mat in range(4):
        cut(4 + mat, mat)
    for step in range(I_STEPS):
        if step >= N:
            directions(step - N)
        take(step, 0)
        if step >= N:
            cosines(step - N)
        take(step, 1)
        if step > N:
            sup_lo(step - N - 1)
        take(step, 2)
        take(step, 3)
        if step + 2 < I_STEPS:
            for mat in range(2):
                cut(8 + 2 * step + mat, 2 * (step % 2) + mat)
        if step == I_STEPS - 2:
            for mat in range(2):
                cut(20 + mat, mat)
        if step >= N:
            superpose(step - N)
    for mat in range(2):
        cut(22 + mat, 2 + mat)
    cut(24, 4, 1)
    for x, part in ((4, measure), (5, post), (6, top)):
        sup_lo(x - 1)
        directions(x)
        cosines(x)
        superpose(x)
        part(0)
    directions(7)
    sup_lo(6)
    cosines(7)
    superpose(7)
    sup_lo(7)
    for part in (measure, post, top):
        part(1)


def final_pool(nc, pool, io, m, s):
    def store(k):
        step, k4 = divmod(k, 4)
        half, n = divmod(step, N)
        pool.wait_ge(s.r_done, k + 1)
        pool.wait_ge(s.i_out, k + 1)
        pool.dma_start(io.ri_scr[half * ROWS + k4, :, n, :], m.stage[:, k % 2, :]).then_inc(s.ri_stored[k % 2], 16)

    def load(x):
        if x % ROWS == 0:
            for e in range(2):
                pool.wait_ge(s.ri_stored[e], 16 * (I_TILES // 4) * (x // ROWS + 1))
        if x:
            pool.wait_ge(s.fz_done, x)
        pool.dma_start(m.ri[:, :], io.ri_scr[x].rearrange("p n w -> p (n w)")).then_inc(s.ri_loaded, 16)

    def zeros(x):
        pool.wait_ge(s.x_zero, x + 1)
        pool.wait_ge(s.u_done, x + 1)
        zero = m.zero[:, :].rearrange("p (n d) -> p n d", n=N)
        zp = m.n2[:, 0:1536].bitcast(BF16).rearrange("p (a d) -> p a d", d=D)
        for n, (i, j) in enumerate(PAIRS_OF_N):
            nc.gpsimd.tensor_tensor(zp[:, n], zero[:, i], zero[:, j], ALU.add).then_inc(s.zero_pairs, 1)

    def load_top(h, j):
        v = h * C + j
        if v >= 2:
            pool.wait_ge(s.h1_lo, v - 1)
        if h and j == 0:
            pool.wait_ge(s.y_stored, 16)
        pool.dma_start(m.top_x[:, j % 2, :], io.top_scr[j, :, bass.ts(h, HALF)]).then_inc(s.top_x_loaded[j % 2], 16)

    pool.wait_ge(s.attn_done, 2 * C * TILES)
    pool.wait_ge(s.stored_top, 16 * C * HALVES)
    for k in range(I_TILES):
        if k == I_TILES // 2:
            load(0)
        store(k)
        if k >= I_TILES // 2 and k % 4 == 0:
            zeros((k - I_TILES // 2) // 4)
        if k >= I_TILES // 2 and k % 4 == 3:
            load((k - I_TILES // 2) // 4 + 1)
    for e in range(2):
        pool.wait_ge(s.ri_stored[e], 16 * I_TILES // 2)
    pool.dma_start(m.mean_of_out[:, :], io.mean_of_out).then_inc(s.mean_loaded, 16)
    for x in range(ROWS, TILES):
        zeros(x)
        if x + 1 < TILES:
            load(x + 1)
        if x == 6:
            for j in range(C):
                load_top(0, j)
    for j in range(C):
        load_top(1, j)


def gather_strengths(nc, pool, io, m, s):
    pool.dma_start(m.ids[:, :], io.ids).then_inc(s.ids_loaded, 16)
    pool.wait_ge(s.ids_loaded, 16)
    for x in range(TILES):
        for f, table in enumerate(io.tables):
            nc.gpsimd.indirect_dma_start(
                out=m.strength[:, x, N * f:N * f + N], out_offset=None, in_=table,
                in_offset=bass.IndirectOffsetOnAxis(ap=m.ids[:, x * N + f:x * N + f + 1], axis=0),
            ).then_inc(s.strength_loaded, 16)


LATE_DMAS = 3


class Names:
    pass


def name_semaphores(nc, ctx):
    s = Names()

    def one(name):
        return ctx.enter_context(nc.semaphore(name))

    def two(name):
        return [one(name + "0"), one(name + "1")]

    s.aiwi_out = one("aiwi_out")
    s.amp_hi = one("amp_hi")
    s.amp_lo = one("amp_lo")
    s.amp_root = one("amp_root")
    s.amp_sq = one("amp_sq")
    s.at_hi = one("at_hi")
    s.at_lo = one("at_lo")
    s.at_stored = two("at_stored")
    s.attn_done = one("attn_done")
    s.bias_done = one("bias_done")
    s.block_done = one("block_done")
    s.bo_done = one("bo_done")
    s.bv_done = one("bv_done")
    s.compacted = one("compacted")
    s.consts_loaded = one("consts_loaded")
    s.cos_done = one("cos_done")
    s.evac_act = one("evac_act")
    s.evac_dve = one("evac_dve")
    s.exp_done = one("exp_done")
    s.f_done = one("f_done")
    s.fz_done = one("fz_done")
    s.gathered = one("gathered")
    s.gelu_done = one("gelu_done")
    s.h1_hi = one("h1_hi")
    s.h1_lo = one("h1_lo")
    s.h2_done = one("h2_done")
    s.h2_part = one("h2_part")
    s.half_sum = one("half_sum")
    s.hi_done = one("hi_done")
    s.i_done = one("i_done")
    s.i_out = one("i_out")
    s.ids_loaded = one("ids_loaded")
    s.inverse_done = one("inverse_done")
    s.late_loaded = one("late_loaded")
    s.lo_done = one("lo_done")
    s.mag2_done = one("mag2_done")
    s.mag_done = one("mag_done")
    s.masked = one("masked")
    s.max_done = one("max_done")
    s.mean_loaded = one("mean_loaded")
    s.mean_sq = one("mean_sq")
    s.means_done = one("means_done")
    s.measured = one("measured")
    s.mi_sq = one("mi_sq")
    s.misi_out = one("misi_out")
    s.mr_done = one("mr_done")
    s.mr_sq = one("mr_sq")
    s.nki_done = one("nki_done")
    s.norm_centred = one("norm_centred")
    s.norm_eps = one("norm_eps")
    s.norm_hi = one("norm_hi")
    s.norm_inverse = one("norm_inverse")
    s.norm_lo = one("norm_lo")
    s.norm_root = one("norm_root")
    s.norm_scaled = one("norm_scaled")
    s.norm_sum = one("norm_sum")
    s.ot_hi = one("ot_hi")
    s.ot_lo = one("ot_lo")
    s.pair_mul = one("pair_mul")
    s.pair_sum = one("pair_sum")
    s.posted = one("posted")
    s.pre_added = one("pre_added")
    s.pre_done = one("pre_done")
    s.projected = one("projected")
    s.qk_hi = one("qk_hi")
    s.qk_lo = one("qk_lo")
    s.quarter_loaded = two("quarter_loaded")
    s.r_done = one("r_done")
    s.raw_loaded = two("raw_loaded")
    s.ri_loaded = one("ri_loaded")
    s.ri_stored = two("ri_stored")
    s.rstd_done = one("rstd_done")
    s.scored = one("scored")
    s.shifted = one("shifted")
    s.softmaxed = one("softmaxed")
    s.spread_done = one("spread_done")
    s.sq_added = one("sq_added")
    s.sq_done = one("sq_done")
    s.std_done = one("std_done")
    s.stored = one("stored")
    s.stored_top = one("stored_top")
    s.strength_loaded = one("strength_loaded")
    s.sums_ready = one("sums_ready")
    s.sup_done = one("sup_done")
    s.sup_hi = one("sup_hi")
    s.sup_lo = one("sup_lo")
    s.sup_sum = one("sup_sum")
    s.table_loaded = one("table_loaded")
    s.tile_loaded = two("tile_loaded")
    s.top_sum = one("top_sum")
    s.top_x_loaded = two("top_x_loaded")
    s.topped = one("topped")
    s.total_done = one("total_done")
    s.turned = one("turned")
    s.u_done = one("u_done")
    s.v_done = one("v_done")
    s.v_hi = one("v_hi")
    s.v_lo = one("v_lo")
    s.v_tile_loaded = one("v_tile_loaded")
    s.var_done = one("var_done")
    s.var_raw = one("var_raw")
    s.weighed = one("weighed")
    s.wf_hi = one("wf_hi")
    s.wf_lo = one("wf_lo")
    s.wt_done = one("wt_done")
    s.wt_hi = one("wt_hi")
    s.wt_lo = one("wt_lo")
    s.x_clamped = one("x_clamped")
    s.x_inverse = one("x_inverse")
    s.x_root = one("x_root")
    s.x_sq = one("x_sq")
    s.x_sum = one("x_sum")
    s.x_zero = one("x_zero")
    s.y_done = one("y_done")
    s.y_out = one("y_out")
    s.y_stored = one("y_stored")
    s.z_added = one("z_added")
    s.z_centred = one("z_centred")
    s.z_gelu = one("z_gelu")
    s.z_hi = one("z_hi")
    s.z_lo = one("z_lo")
    s.z_mean_sq = one("z_mean_sq")
    s.z_means = one("z_means")
    s.z_pre = one("z_pre")
    s.z_rstd = one("z_rstd")
    s.z_scaled = one("z_scaled")
    s.z_sq = one("z_sq")
    s.z_sq_added = one("z_sq_added")
    s.z_std = one("z_std")
    s.z_sums = one("z_sums")
    s.z_var = one("z_var")
    s.z_var_raw = one("z_var_raw")
    s.zero_pairs = one("zero_pairs")
    return s




def place_memory(nc, ctx):
    m = Names()

    def sb(shape, name, dt=F32, stack=ctx):
        return stack.enter_context(nc.sbuf_tensor(name, shape, dt))

    m.x = sb([P, 2, KC * HALF], "x", F32R)
    m.h = sb([P, 2, KC * HALF], "h", F32R)
    m.params = sb([P, PARAMS], "params")
    m.table = sb([P, P], "table")
    m.strength = sb([P, TILES, N * N], "strength")
    m.raw = sb([P, 2, UNIT], "raw")
    with ExitStack() as e:
        m.pre = sb([P, KC * HALF], "pre", stack=e)
        m.ws = sb([P, 2, 2, 2, UNIT], "ws", F32R, e)
        m.tmp = sb([P, 2, HALF], "tmp", stack=e)
        m.ids = sb([P, TILES * N], "ids", I32, e)
    with ExitStack() as qv:
        m.weights = sb([P, TILES * P], "weights", stack=qv)
        m.own_row = sb([P, 32], "own_row", stack=qv)
        m.own_n = sb([P, N], "own_n", stack=qv)
        m.select = sb([P, N, P], "select", stack=qv)
        with ExitStack() as q:
            m.qk = sb([P, QK_BUFS, 5, 2, 512], "qk", F32R, q)
            m.masked = sb([P, 4, 512], "masked", stack=q)
            m.compact = sb([P, PAIRS, 2, 2, 16], "compact", stack=q)
            m.squares = sb([P, 256], "squares", stack=q)
            m.mag2 = sb([P, P], "mag2", stack=q)
            m.mag = sb([P, P], "mag", stack=q)
            m.top = sb([P, 32], "top", stack=q)
            m.total = sb([P, 32], "total", stack=q)
            m.inverse = sb([P, 32], "inverse", stack=q)
        with ExitStack() as v:
            m.v = sb([P, 2, 2, 2, D], "v", F32R, v)
            m.wf = sb([P, 2, HEADS * P], "wf", F32R, v)
            m.ot = sb([P, 2, 2, PAIRS, 512], "ot", F32R, v)
            m.wt = sb([P, 2, P], "wt", F32R, v)
            m.spread = sb([P, N, P], "spread", stack=v)
            m.bv = sb([P, 2, PAIRS, 2], "bv", F32R, v)
            m.bo = sb([P, 2 * C], "bo", stack=v)
    m.ri = sb([P, 2 * N * D], "ri")
    m.u = sb([P, 2 * N * D], "u")
    m.sq = sb([P, 2 * N * D], "sq")
    m.n2 = sb([P, N * D], "n2")
    m.zero = sb([P, N * D], "zero", BF16)
    m.norms = sb([P, 4], "norms")
    with ExitStack() as i:
        m.stage = sb([P, 2, 1024], "stage", stack=i)
        m.aiwi = sb([P, 512], "aiwi", stack=i)
    m.top_x = sb([P, 2, HALF], "top_x")
    m.pair = sb([P, 2, HALF], "pair")
    m.mean_of_out = sb([P, P], "mean_of_out")
    m.a = m.h[:, 0, 0:4096].rearrange("p (b w) -> p b w", b=2)
    m.h1 = m.h[:, 0, 4096:6144].rearrange("p (k b w) -> p k b w", k=2, b=2)
    m.top2 = m.h[:, 0, 6144:8192].rearrange("p (b w) -> p b w", b=2)
    m.acc = ctx.enter_context(nc.psum_tensor("acc", [P, 4, 512], F32))
    m.stat = ctx.enter_context(nc.psum_tensor("stat", [P, 4, 512], F32))
    m.mean, m.rstd, m.sums, m.sums_sq = (m.stat[:, i, :] for i in range(4))
    return m


def program(nc, io):
    with ExitStack() as ctx:
        m, s = place_memory(nc, ctx), name_semaphores(nc, ctx)
        block = ctx.enter_context(nc.Block())

        @block.sync
        def _(sp):
            encoder_loads(nc, sp, io, m, s)
            scores_sync(nc, sp, io, m, s)
            values_sync(nc, sp, io, m, s)
            final_sync(nc, sp, io, m, s)

        @block.scalar
        def _(act):
            act.dma_start(m.params[:, :], io.params).then_inc(s.consts_loaded, 16)
            act.dma_start(m.table[:, :], io.mean_of_hid).then_inc(s.consts_loaded, 16)
            act.wait_ge(s.consts_loaded, 32)
            encoder_scalar(nc, act, io, m, s)
            qk_scalar(nc, act, io, m, s)
            values_scalar(nc, act, io, m, s)
            final_scalar(nc, act, io, m, s)

        @block.vector
        def _(dve):
            dve.wait_ge(s.consts_loaded, 32)
            encoder_vector(nc, dve, io, m, s)
            qk_vector(nc, dve, io, m, s)
            values_vector(nc, dve, io, m, s)
            final_vector(nc, dve, io, m, s)

        @block.tensor
        def _(pe):
            pe.wait_ge(s.consts_loaded, 32)
            encoder_tensor(nc, pe, io, m, s)
            scores_tensor(nc, pe, io, m, s)
            values_tensor(nc, pe, io, m, s)
            pe.wait_ge(s.table_loaded, 16)
            final_tensor(nc, pe, io, m, s)

        @block.gpsimd
        def _(pool):
            gather_strengths(nc, pool, io, m, s)
            encoder_stores(nc, pool, io, m, s)
            pool.wait_ge(s.strength_loaded, 16 * TILES * N)
            pool.wait_ge(s.norm_lo, 32 * HALVES)
            pool.dma_start(m.own_row[:, :], io.own_row).then_inc(s.late_loaded, 16)
            pool.dma_start(m.own_n[:, :], io.own_n).then_inc(s.late_loaded, 16)
            pool.dma_start(m.select[:, :, :], io.select).then_inc(s.late_loaded, 16)
            pool.wait_ge(s.means_done, 2 * HALVES)
            pool.dma_start(m.table[:, :], io.identity).then_inc(s.table_loaded, 16)
            values_pool(nc, pool, io, m, s)
            final_pool(nc, pool, io, m, s)



def kernel(**inputs):
    import numpy as _np
    import concourse.bacc as _bacc
    from concourse import mybir as _mybir
    from concourse.bass_utils import run_bass_kernel_spmd as _run

    nc = _bacc.Bacc("TRN2", target_bir_lowering=False, num_devices=1)
    arrays, io = {}, Names()
    given = {k.replace("L0_rec_", ""): _np.asarray(v) for k, v in inputs.items()}

    def give(name, array):
        array = _np.ascontiguousarray(array)
        arrays["in_" + name] = array
        return nc.dram_tensor("in_" + name, array.shape, _mybir.dt.from_np(array.dtype), kind="ExternalInput").ap()

    def scratch(name, shape):
        return nc.dram_tensor(name, shape, _mybir.dt.float32, kind="Internal").ap()

    def narrow(w):
        k, n = w.shape
        return w.reshape(k // UNIT, UC, P, n // P, P).transpose(3, 0, 2, 1, 4).reshape(-1, P, UNIT)

    def wide(w):
        return w.reshape(C, P, -1).transpose(1, 0, 2).reshape(P, -1, UNIT).transpose(1, 0, 2)

    x = given["r_x"].T
    x_halves = [x[:, k * HALF:(k + 1) * HALF].reshape(X_UNITS, 2, P, HALF).transpose(0, 2, 1, 3).reshape(X_UNITS, P, UNIT)
                for k in range(HALVES)]
    z_features = D
    io.w_units = give("w_units", _np.concatenate([narrow(given[k].T) for k in ("er_W1", "ei_W1", "er_W2", "ei_W2")]
                                    + [narrow(given["W_top1"][z_features:])]))
    io.x_units = give("x_units", _np.concatenate(x_halves + [wide(given[k].T) for k in ("Wq_r", "Wq_i", "Wk_r", "Wk_i")]))
    late = [given[k].T for k in ("Wv_r", "Wv_i", "Wo_r", "Wo_i")]
    for n in range(N):
        late += [given["int_Wr"][n].T, given["int_Wi"][n].T]
    late += [given["meas_Mr"].T, given["meas_Mi"].T, given["post_W"].T, given["W_top1"][:z_features], given["W_top2"]]
    io.late_units = give("late_units", _np.concatenate([wide(w) for w in late]))
    columns = ("er_b1", "er_g1", "er_be1", "ei_b1", "ei_g1", "ei_be1", "er_b2", "ei_b2", "b_top1", "bq_r", "bq_i", "bk_r",
               "bk_i", "bv_r", "bv_i", "bo_r", "bo_i", "post_b", "post_g", "post_be", "b_top2", "W_top3")
    io.params = give("params", _np.concatenate([given[k].reshape(-1, P).T for k in columns], axis=1))
    io.ids = give("ids", given["ids"].reshape(TILES, P, N).transpose(1, 0, 2).reshape(P, TILES * N))
    io.tables = [give("tbl_" + str(f), given["tbl_" + str(f)]) for f in range(N)]
    p = _np.arange(P)
    f32 = _np.float32
    io.mean_of_hid = give("mean_of_hid", _np.full((P, P), 1.0 / HID, f32))
    io.mean_of_out = give("mean_of_out", _np.full((P, P), 1.0 / D, f32))
    io.identity = give("identity", _np.eye(P, dtype=f32))
    io.own_row = give("own_row", (p[:, None] % 32 == _np.arange(32)).astype(f32))
    io.own_n = give("own_n", (p[:, None] // 32 == _np.arange(N)).astype(f32))
    io.select = give("select", ((p[:, None, None] % 32 == p % 32) & (p // 32 == _np.arange(N)[:, None])).astype(f32))
    io.s_scr = scratch("s_scr", (2, 2, N, C, P, BATCH))
    io.top_scr = scratch("top_scr", (C, P, BATCH))
    io.a_scr = scratch("a_scr", (2, 2, N, C, P, BATCH))
    io.ri_scr = scratch("ri_scr", (TILES, P, N, 2 * D))
    io.y = nc.dram_tensor("out_y", (HALVES, HALF), _mybir.dt.float32, kind="ExternalOutput").ap()
    program(nc, io)
    result = _run(nc, [arrays], core_ids=[0])
    return result.results[0]["out_y"].reshape(BATCH, 1)
```

```python
from contextlib import ExitStack

import concourse.bass as bass
from concourse import mybir

F32 = mybir.dt.float32
F32R = mybir.dt.float32r
I32 = mybir.dt.int32
BF16 = mybir.dt.bfloat16
U8 = mybir.dt.uint8
ACT = mybir.ActivationFunctionType
ALU = mybir.AluOpType
AX = mybir.AxisListType

P = 128
BATCH, IN, HID, D, N = 1024, 2048, 2048, 512, 4
HEADS, HD = 8, 64
HALF = 512
HALVES = BATCH // HALF
KC = IN // P
C = D // P
UC = 8
UNIT = UC * P
BLOCKS = {"W1r": 16, "W1i": 16, "W2r": 16, "top": 4, "W2i": 16}
FIRST_UNIT = {"W1r": 0, "W1i": 32, "W2r": 64, "W2i": 96, "top": 128}
JOBS = ["W1r", "W1i", "W2r", "top", "W2i"]
START = {j: sum(BLOCKS[k] for k in JOBS[:n]) for n, j in enumerate(JOBS)}
PER_HALF = sum(BLOCKS.values())
X_UNITS = 8
X_STEPS = range(2, 6)
LN_EPS = 1e-5
TILES = BATCH // P


PARAM = {}
_at = 0
for _name, _n in (("r_b1", 16), ("r_g1", 16), ("r_be1", 16), ("i_b1", 16), ("i_g1", 16), ("i_be1", 16),
                  ("r_b2", 16), ("i_b2", 16), ("top1", 4), ("q_r", 4), ("q_i", 4), ("k_r", 4), ("k_i", 4),
                  ("v_r", 4), ("v_i", 4), ("o_r", 4), ("o_i", 4),
                  ("post_b", 4), ("post_g", 4), ("post_be", 4), ("top2", 2), ("w3", 2), ("tiny", 1), ("norm_eps", 1)):
    PARAM[_name] = _at
    _at += _n
PARAMS = _at



def act_bias(params, name, index):
    return params[:, bass.ds(PARAM[name] + index, 1)]


def pair_of(half, job, b, with_x=0):
    return X_UNITS // 2 + half * (PER_HALF + X_UNITS // 2) + START[job] + b + with_x


def block_of(half, job, b):
    return half * PER_HALF + START[job] + b


def w2_block_of(half, job, b):
    return half * 32 + (16 if job == "W2i" else 0) + b


def w1_block_of(half, job, b):
    return half * 32 + (16 if job == "W1i" else 0) + b


def before(half, job, s):
    if not isinstance(s, int) or s >= 2:
        return half, job, s - 2
    n = JOBS.index(job)
    if n:
        return half, JOBS[n - 1], BLOCKS[JOBS[n - 1]] - 2 + s
    return (half - 1, JOBS[-1], BLOCKS[JOBS[-1]] - 2 + s) if half else None


def after(half, job, s):
    if not isinstance(s, int) or s + 1 < BLOCKS[job]:
        return half, job, s + 1
    n = JOBS.index(job)
    if n + 1 < len(JOBS):
        return half, JOBS[n + 1], 0
    return (half + 1, JOBS[0], 0) if half + 1 < HALVES else None


def x_pairs(job, b):
    if job != "W2i" or (isinstance(b, int) and b <= 3):
        return 0
    return min(b - 3, 4) if isinstance(b, int) else 4


def steps(eng, job, do):
    head = 6 if job == "W2i" else 4
    for b in range(head):
        do(b, b % 4)
    with eng.Fori(0, 2) as i:
        for k in range(4):
            do(i * 4 + (head + k), (head + k) % 4)
    for b in range(head + 8, 16):
        do(b, b % 4)


def encoder_loads(nc, sp, io, m, s):
    def pair(q, src, first):
        for k in range(2):
            if not isinstance(q, int) or q >= 1:
                sp.wait_ge(s.lo_done, q * 2 + (k - 1))
            sp.dma_start(m.raw[:, k, :], src[first + k]).then_inc(s.raw_loaded[k], 16)

    for q in range(4):
        pair(q, io.x_units, 2 * q)
    for half in range(HALVES):
        for job in JOBS:
            def load(b, with_x):
                pair(pair_of(half, job, b, with_x), io.w_units, b * 2 + FIRST_UNIT[job])

            if job != "W2i":
                with sp.Fori(0, BLOCKS[job]) as b:
                    load(b, 0)
                continue
            with sp.Fori(0, 4) as b:
                load(b, 0)
            for n in range(4):
                pair(pair_of(half, job, 4 + n, n), io.x_units, X_UNITS * (half + 1) + 2 * n)
                if n < 3:
                    load(4 + n, n + 1)
            with sp.Fori(7, 16) as b:
                load(b, 4)


def cut_hi(nc, act, m, s, q, dst, k):
    act.wait_ge(s.raw_loaded[k], (q + 1) * 16)
    nc.scalar.copy(dst[0], m.raw[:, k, :]).then_inc(s.hi_done, 1)


def cut_lo(nc, dve, m, s, q, dst, k):
    dve.wait_ge(s.hi_done, q * 2 + (k + 1))
    nc.vector.tensor_tensor(dst[1], m.raw[:, k, :], dst[0].bitcast(F32), ALU.subtract).then_inc(s.lo_done, 1)


def w_slot(m, parity, k):
    return [m.ws[:, parity, k, part, :] for part in range(2)]


def x_slot(m, n):
    return [m.x[:, part, bass.ts(n, UNIT)] for part in range(2)]


def encoder_scalar(nc, act, io, m, s):
    for q in range(4):
        for k in range(2):
            cut_hi(nc, act, m, s, q, x_slot(m, 2 * q + k), k)
    for k in range(2):
        cut_hi(nc, act, m, s, 4, w_slot(m, 0, k), k)

    for half in range(HALVES):
        for job in JOBS:
            def step(b, phase, between=None):
                nxt = after(half, job, b)
                if nxt:
                    w = block_of(*nxt)
                    if not isinstance(w, int) or w >= 2:
                        act.wait_ge(s.block_done, w - 1)
                    q = pair_of(nxt[0], nxt[1], nxt[2], x_pairs(nxt[1], nxt[2]))
                    for k in range(2):
                        cut_hi(nc, act, m, s, q, w_slot(m, (phase + 1) % 2, k), k)
                if between:
                    between()
                old = before(half, job, b)
                if old:
                    take_out(old, (phase - 2) % 4)
                if job == "W2i" and isinstance(b, int) and b in X_STEPS:
                    n = b - X_STEPS[0]
                    for k in range(2):
                        cut_hi(nc, act, m, s, pair_of(half, job, b + 2, n), x_slot(m, 2 * n + k), k)

            def take_out(old, bank):
                oh, oj, ob = old
                acc = m.acc[:, bank, :]
                w = block_of(oh, oj, ob)
                act.wait_ge(s.block_done, w + 1)
                if oj in ("W1r", "W1i"):
                    bias = act_bias(m.params, oj[2] + "_b1", ob)
                    u = w1_block_of(oh, oj, ob)
                    if oh or oj == "W1i":
                        act.wait_ge(s.norm_lo, u - 15)
                    if not isinstance(u, int) or u % 16 >= 2:
                        act.wait_ge(s.sq_added, u - 1)
                    elif u >= 16:
                        act.wait_ge(s.rstd_done, u // 16)
                        if u == 32:
                            act.wait_ge(s.stored, 32 * 32)
                    nc.scalar.activation(m.pre[:, bass.ts(ob, HALF)], acc, ACT.Identity, bias=bias).then_inc(s.pre_done, 1)
                    nc.scalar.activation(m.tmp[:, bank % 2, :], acc, ACT.Square, bias=bias).then_inc(s.evac_act, 1)
                elif oj == "top":
                    t = oh * 4 + ob
                    act.wait_ge(s.stored, 32 * w2_block_of(oh, "W2i", 0))
                    if t >= 1:
                        act.wait_ge(s.stored_top, 16 * t)
                    nc.scalar.activation(m.tmp[:, 0, :], acc, ACT.Identity,
                                         bias=act_bias(m.params, "top1", ob)).then_inc(s.evac_act, 1)
                else:
                    v = w2_block_of(oh, oj, ob)
                    if oj == "W2i" and isinstance(ob, int) and ob == 0:
                        act.wait_ge(s.stored_top, 16 * 4 * (oh + 1))
                    if not isinstance(v, int) or v >= 1:
                        act.wait_ge(s.stored, v * 32)
                    if oj == "W2r" and isinstance(ob, int) and ob == 0:
                        act.wait_ge(s.rstd_done, 2 * oh + 2)
                    nc.scalar.activation(m.tmp[:, 0, :].bitcast(F32R), acc, ACT.Identity,
                                         bias=act_bias(m.params, oj[2] + "_b2", ob)).then_inc(s.evac_act, 1)

            def normalise(b, n):
                enc = "r" if job == "W1i" else "i"
                act.wait_ge(s.block_done, block_of(half, "top" if job == "top" else "W1r", 0))
                for j in range(2):
                    act.wait_ge(s.norm_scaled, n + (j + 1))
                    cols = bass.ts(b + j, HALF)
                    nc.scalar.activation(m.pre[:, cols], m.pre[:, cols], ACT.Gelu,
                                         bias=act_bias(m.params, enc + "_be1", b + j),
                                         scale=act_bias(m.params, enc + "_g1", b + j)).then_inc(s.gelu_done, 1)
                    act.wait_ge(s.gelu_done, n + (j + 1))
                    nc.scalar.copy(m.h[:, 0, cols], m.pre[:, cols]).then_inc(s.norm_hi, 1)

            def deviation(r):
                act.wait_ge(s.means_done, r + 1)
                nc.scalar.activation(m.tmp[:, 0, :], m.mean, ACT.Square).then_inc(s.mean_sq, 1)
                act.wait_ge(s.var_done, r + 1)
                nc.scalar.activation(m.tmp[:, 0, :], m.tmp[:, 1, :], ACT.Sqrt).then_inc(s.std_done, 1)

            job_steps(act, half, job, step, lambda b, n: None, normalise, deviation)
    for b in (14, 15):
        take_out((HALVES - 1, "W2i", b), b % 4)


def job_steps(eng, half, job, step, scale, normalise, deviation):
    if job == "W1i":
        first = half * 32
        step(0, 0)
        step(1, 1)
        deviation(2 * half)
        for b in range(2, 16):
            step(b, b % 4, (lambda: normalise(2 * (b - 2), first + 2 * (b - 2))) if b < 10 else None)
    elif job == "top":
        first = half * 32 + 16
        for b in range(4):
            step(b, b)
            with eng.Fori(0, 2) as i:
                normalise(i * 2 + 4 * b, i * 2 + (first + 4 * b))
    elif job == "W2r":
        def with_scaling(b, phase):
            step(b, phase)
            if isinstance(b, int) and b == 1:
                deviation(2 * half + 1)
            if not isinstance(b, int):
                scale(b * 2 - 8, b * 2 + (half * 32 + 16 - 8))

        steps(eng, job, with_scaling)
    else:
        steps(eng, job, step)


def encoder_vector(nc, dve, io, m, s):
    for q in range(4):
        for k in range(2):
            cut_lo(nc, dve, m, s, q, x_slot(m, 2 * q + k), k)
    for k in range(2):
        cut_lo(nc, dve, m, s, 4, w_slot(m, 0, k), k)

    for half in range(HALVES):
        for job in JOBS:
            def step(b, phase, between=None):
                nxt = after(half, job, b)
                if nxt:
                    q = pair_of(nxt[0], nxt[1], nxt[2], x_pairs(nxt[1], nxt[2]))
                    for k in range(2):
                        cut_lo(nc, dve, m, s, q, w_slot(m, (phase + 1) % 2, k), k)
                if between:
                    between()
                old = before(half, job, b)
                if old:
                    take_out(old, (phase - 2) % 4)
                if job == "W2i" and isinstance(b, int) and b in X_STEPS:
                    n = b - X_STEPS[0]
                    for k in range(2):
                        cut_lo(nc, dve, m, s, pair_of(half, job, b + 2, n), x_slot(m, 2 * n + k), k)

            def take_out(old, bank):
                oh, oj, ob = old
                if oj == "top":
                    return
                w = block_of(oh, oj, ob)
                if oj in ("W1r", "W1i"):
                    u = w1_block_of(oh, oj, ob)
                    start = isinstance(ob, int) and ob == 0
                    dve.wait_ge(s.pre_done, u + 1)
                    pre, sq = m.pre[:, bass.ts(ob, HALF)], m.tmp[:, bank % 2, :]
                    if start:
                        nc.vector.tensor_copy(m.sums, pre).then_inc(s.pre_added, 1)
                    else:
                        dve.wait_ge(s.pre_added, u)
                        nc.vector.tensor_tensor(m.sums, m.sums, pre, ALU.add).then_inc(s.pre_added, 1)
                    dve.wait_ge(s.evac_act, w + 1)
                    if start:
                        nc.vector.tensor_copy(m.sums_sq, sq).then_inc(s.sq_added, 1)
                    else:
                        dve.wait_ge(s.sq_added, u)
                        nc.vector.tensor_tensor(m.sums_sq, m.sums_sq, sq, ALU.add).then_inc(s.sq_added, 1)
                    if isinstance(ob, int) and ob == 15:
                        r = u // 16
                        dve.wait_ge(s.pre_added, u + 1)
                        dve.wait_ge(s.sq_added, u + 1)
                        nc.vector.tensor_copy(m.tmp[:, 0, :], m.sums).then_inc(s.sums_ready, 1)
                        nc.vector.tensor_copy(m.tmp[:, 1, :], m.sums_sq).then_inc(s.sums_ready, 1)
                else:
                    v = w2_block_of(oh, oj, ob)
                    dve.wait_ge(s.evac_act, w + 1)
                    if not isinstance(v, int) or v >= 1:
                        dve.wait_ge(s.stored, v * 32)
                    nc.vector.scalar_tensor_tensor(
                        out=m.tmp[:, 1, :].bitcast(F32R), in0=m.acc[:, bank, :],
                        scalar=act_bias(m.params, oj[2] + "_b2", ob), in1=m.tmp[:, 0, :],
                        op0=ALU.add, op1=ALU.subtract).then_inc(s.evac_dve, 1)

            def scale(b, n):
                for j in range(2):
                    cols = bass.ts(b + j, HALF)
                    nc.vector.tensor_tensor(m.pre[:, cols], m.pre[:, cols], m.mean, ALU.subtract).then_inc(s.norm_centred, 1)
                    dve.wait_ge(s.norm_centred, n + (j + 1))
                    nc.vector.tensor_tensor(m.pre[:, cols], m.pre[:, cols], m.rstd, ALU.mult).then_inc(s.norm_scaled, 1)

            def normalise(b, n):
                if job == "W1i":
                    scale(b, n)
                for j in range(2):
                    cols = bass.ts(b + j, HALF)
                    dve.wait_ge(s.norm_hi, n + (j + 1))
                    nc.vector.tensor_tensor(m.h[:, 1, cols], m.pre[:, cols], m.h[:, 0, cols].bitcast(F32),
                                            ALU.subtract).then_inc(s.norm_lo, 1)

            def deviation(r):
                dve.wait_ge(s.mean_sq, r + 1)
                nc.vector.tensor_tensor(m.tmp[:, 1, :], m.rstd, m.tmp[:, 0, :], ALU.subtract).then_inc(s.var_raw, 1)
                dve.wait_ge(s.var_raw, r + 1)
                nc.vector.tensor_scalar(m.tmp[:, 1, :], m.tmp[:, 1, :], 0.0, LN_EPS, ALU.max, ALU.add).then_inc(s.var_done, 1)
                dve.wait_ge(s.std_done, r + 1)
                nc.vector.reciprocal(m.rstd, m.tmp[:, 0, :]).then_inc(s.rstd_done, 1)
                dve.wait_ge(s.rstd_done, r + 1)

            job_steps(dve, half, job, step, scale, normalise, deviation)
    for b in (14, 15):
        take_out((HALVES - 1, "W2i", b), b % 4)


def product(nc, out, stationary, moving, start, stop):
    nc.tensor.matmul(out, stationary[0], moving[0], start=start, stop=False)
    nc.tensor.matmul(out, stationary[0], moving[1], start=False, stop=False)
    return nc.tensor.matmul(out, stationary[1], moving[0], start=False, stop=stop)


def encoder_tensor(nc, pe, io, m, s):
    def means(r):
        pe.wait_ge(s.sums_ready, 2 * r + 2)
        nc.tensor.matmul(m.mean, m.table[:, :], m.tmp[:, 0, :], start=True, stop=True)
        nc.tensor.matmul(m.rstd, m.table[:, :], m.tmp[:, 1, :], start=True, stop=True).then_inc(s.means_done, 1)

    for half in range(HALVES):
        for job in JOBS:
            src = m.h if job[:2] == "W2" else m.x

            def compute(b, phase, with_x):
                w = block_of(half, job, b)
                if not isinstance(b, int) or b >= 4:
                    free = (half, job, b - 4)
                else:
                    free = (half, job, b)
                    n = JOBS.index(job)
                    prev = JOBS[n - 1]
                    free = (half if n else half - 1, prev, BLOCKS[prev] - 4 + b)
                if free[0] >= 0:
                    if free[1][:2] == "W2":
                        pe.wait_ge(s.evac_dve, w2_block_of(*free) + 1)
                    else:
                        pe.wait_ge(s.evac_act, block_of(*free) + 1)
                q = pair_of(half, job, b, with_x)
                for k in range(2):
                    pe.wait_ge(s.lo_done, q * 2 + (k + 1))
                    for c in range(UC):
                        if job[:2] == "W2" and isinstance(b, int) and b == 0:
                            pe.wait_ge(s.norm_lo, half * 32 + (16 if job == "W2i" else 0) + UC * k + c + 1)
                        wh, wl = (m.ws[:, phase % 2, k, part, bass.ts(c, P)] for part in range(2))
                        cols = bass.ts(UC * k + c, HALF)
                        last = product(nc, m.acc[:, phase, :], (wh, wl), (src[:, 0, cols], src[:, 1, cols]),
                                       k == 0 and c == 0, k == 1 and c == UC - 1)
                last.then_inc(s.block_done, 1)

            if job == "top":
                for b in range(4):
                    compute(b, b, 0)
                continue
            head = 8 if job == "W2i" else 4
            for b in range(head):
                compute(b, b % 4, x_pairs(job, b))
                if b == 1 and job in ("W1i", "W2r"):
                    means(half * 2 + (job == "W2r"))
            with pe.Fori(0, (16 - head) // 4) as i:
                for k in range(4):
                    compute(i * 4 + (head + k), k, 4 if job == "W2i" else 0)


def encoder_stores(nc, pool, io, m, s):
    for half in range(HALVES):
        toks = bass.ds(half * HALF, HALF)

        def store(ri, b):
            v = half * 32 + ri * 16 + b
            pool.wait_ge(s.evac_dve, v + 1)
            for part in range(2):
                pool.dma_start(io.s_scr[ri, part, :, :, :, toks].rearrange("n c p r -> (n c) p r")[b], m.tmp[:, part, :].bitcast(F32R)).then_inc(s.stored, 16)

        with pool.Fori(0, 16) as b:
            store(0, b)
        for b in range(4):
            pool.wait_ge(s.evac_act, block_of(half, "top", b) + 1)
            pool.dma_start(io.top_scr[b, :, toks], m.tmp[:, 0, :]).then_inc(s.stored_top, 16)
        with pool.Fori(0, 16) as b:
            store(1, b)



QK_BUFS = 2
QR, QI, KI, KR, NKI = range(5)
MATRICES = [(0, QR, "q_r"), (1, QI, "q_i"), (2, KR, "k_r"), (3, KI, "k_i")]
PAIRS = HEADS // 2
STEPS_Q = TILES * PAIRS
GROUPS = 4


def tile_view(m, buf):
    return m.h[:, buf, :].rearrange("p (a b c w) -> p a b c w", a=2, b=2, c=C)


def load_tile(sp, m, scr, buf, t, sem):
    for ri in range(2):
        for part in range(2):
            for c in range(C):
                sp.dma_start(tile_view(m, buf)[:, ri, part, c, :].rearrange("p (n r) -> p n r", n=N).bitcast(F32),
                             scr[ri, part, :, c, :, bass.ts(t, P)].rearrange("n p r -> p n r")).then_inc(sem, 16)


TILE_DMAS = 2 * 2 * C


def rolled(eng, rounds, unroll, do, ahead=0):
    for k in range(unroll):
        do(0, k, True)
    with eng.Fori(1, rounds - 1) as i:
        for k in range(unroll):
            do(i, k, True)
    for k in range(unroll):
        do(rounds - 1, k, k + ahead < unroll)


def from_step(i, k, n):
    return k >= n or not isinstance(i, int) or i > 0


def following(i, k, unroll):
    return (i, k + 1) if k + 1 < unroll else (i + 1, 0)


def scores_sync(nc, sp, io, m, s):
    sp.wait_ge(s.stored, 32 * 32)
    sp.wait_ge(s.block_done, HALVES * PER_HALF)
    for t in range(2):
        load_tile(sp, m, io.s_scr, t, t, s.tile_loaded[t])
    sp.wait_ge(s.stored, 32 * 32 * HALVES)
    with sp.Fori(1, TILES // 2) as i:
        for k in range(2):
            sp.wait_ge(s.projected, i * 32 + (16 * k - 16))
            load_tile(sp, m, io.s_scr, k, i * 2 + k, s.tile_loaded[k])


def scores_tensor(nc, pe, io, m, s):
    def project(i, k):
        j, buf = k % PAIRS, k // PAIRS
        view = tile_view(m, buf)
        if j == 0:
            pe.wait_ge(s.tile_loaded[buf], i * (16 * TILE_DMAS) + 16 * TILE_DMAS)
        for mat, slot, _ in MATRICES:
            if from_step(i, k, 1):
                pe.wait_ge(s.qk_lo, i * 32 + (4 * k + mat - 3))
            for c in range(C):
                st = [m.x[:, part, bass.ds(mat * C * D + c * D + j * P, P)] for part in range(2)]
                mv = [view[:, mat % 2, part, c, :].rearrange("p (n g r) -> p g n r", n=N, g=GROUPS) for part in range(2)]
                last = product(nc, m.acc[:, mat, :], st, mv, c == 0, c == C - 1)
            last.then_inc(s.projected, 1)

    def score(i, k):
        buf = k % QK_BUFS
        pe.wait_ge(s.qk_lo, i * 32 + (4 * k + 4))
        pe.wait_ge(s.nki_done, i * 8 + (k + 1))
        for gp in range(2):
            if from_step(i, k, 1):
                pe.wait_ge(s.masked, i * 32 + (4 * k + 2 * gp - 2))
            for g2 in range(2):
                group = bass.ts(2 * gp + g2, P)
                for a, (slot, first) in enumerate(((QR, KR), (QI, KI))):
                    for b, (ps, pm) in enumerate(((0, 0), (0, 1), (1, 0))):
                        for hh in range(2):
                            part = slice(64 * hh, 64 * hh + 64)
                            st = m.qk[part, buf, slot, ps, group]
                            mv = m.qk[part, buf, first:first + 2, pm, group]
                            last = nc.tensor.matmul(m.stat[:, 2 * gp + hh, bass.ts(g2, 256)], st, mv,
                                                    start=(a == 0 and b == 0), stop=(a == 1 and b == 2))
                            if g2 == 1 and a == 1 and b == 2:
                                last.then_inc(s.scored, 1)

    pe.wait_ge(s.lo_done, 2 * pair_of(HALVES, "W1r", 0))
    pe.wait_ge(s.evac_dve, 32 * HALVES)
    project(0, 0)

    def step(i, k, more):
        if more:
            project(*following(i, k, 8))
        score(i, k)

    rolled(pe, STEPS_Q // 8, 8, step, 1)


def qk_scalar(nc, act, io, m, s):
    act.wait_ge(s.norm_lo, 32 * HALVES)
    act.wait_ge(s.block_done, HALVES * PER_HALF)
    act.wait_ge(s.stored, 32 * 32 * HALVES)

    def hi(i, k):
        buf = k % QK_BUFS
        if from_step(i, k, 2):
            act.wait_ge(s.scored, i * 32 + (4 * k - 4))
        for mat, slot, name in MATRICES:
            act.wait_ge(s.projected, i * 32 + (4 * k + mat + 1))
            nc.scalar.activation(m.qk[:, buf, slot, 0, :], m.acc[:, mat, :], ACT.Identity,
                                 bias=act_bias(m.params, name, k % PAIRS)).then_inc(s.qk_hi, 1)

    hi(0, 0)

    def step(i, k, more):
        if more:
            hi(*following(i, k, 8))
        if k % PAIRS == PAIRS - 1:
            t = i * 2 + k // PAIRS
            act.wait_ge(s.mag2_done, t + 1)
            nc.scalar.activation(m.mag[:, :], m.mag2[:, :], ACT.Sqrt).then_inc(s.mag_done, 1)
            act.wait_ge(s.shifted, t + 1)
            nc.scalar.activation(m.mag2[:, :], m.mag[:, :], ACT.Exp, scale=HD ** -0.5).then_inc(s.exp_done, 1)

    rolled(act, STEPS_Q // 8, 8, step, 1)


def qk_vector(nc, dve, io, m, s):
    dve.wait_ge(s.block_done, HALVES * PER_HALF)
    dve.wait_ge(s.stored, 32 * 32 * HALVES)
    dve.wait_ge(s.late_loaded, 16 * LATE_DMAS)

    def lo(i, k):
        buf = k % QK_BUFS
        for mat, slot, name in MATRICES:
            dve.wait_ge(s.qk_hi, i * 32 + (4 * k + mat + 1))
            nc.vector.scalar_tensor_tensor(out=m.qk[:, buf, slot, 1, :], in0=m.acc[:, mat, :],
                                           scalar=act_bias(m.params, name, k % PAIRS),
                                           in1=m.qk[:, buf, slot, 0, :].bitcast(F32),
                                           op0=ALU.add, op1=ALU.subtract).then_inc(s.qk_lo, 1)
        dve.wait_ge(s.qk_lo, i * 32 + (4 * k + 4))
        nc.vector.tensor_scalar(m.qk[:, buf, NKI, :, :], m.qk[:, buf, KI, :, :].bitcast(F32), -1.0, None,
                                ALU.mult).then_inc(s.nki_done, 1)

    def take_scores(i, k):
        j = k % PAIRS
        for bank in range(4):
            dve.wait_ge(s.scored, i * 32 + (4 * k + bank + 1))
            if from_step(i, k, 1):
                dve.wait_ge(s.compacted, i * 32 + (4 * k + bank - 3))
            nc.vector.tensor_tensor(m.masked[:, bank, :].rearrange("p (a r) -> p a r", r=32),
                                    m.stat[:, bank, :].rearrange("p (a r) -> p a r", r=32),
                                    m.own_row[:, None, :].to_broadcast([P, 16, 32]), ALU.mult).then_inc(s.masked, 1)
        for bank in range(4):
            gp, hh = bank // 2, bank % 2
            dve.wait_ge(s.masked, i * 32 + (4 * k + bank + 1))
            nc.vector.tensor_reduce(m.compact[:, j, hh, gp, :], m.masked[:, bank, :].rearrange("p (a r) -> p a r", r=32),
                                    AX.X, ALU.add).then_inc(s.compacted, 1)

    def softmax(i, k):
        t = i * 2 + k // PAIRS
        flat = m.compact.rearrange("p j h g w -> p (j h g w)")
        dve.wait_ge(s.compacted, t * 16 + 16)
        nc.vector.tensor_tensor(m.squares[:, :], flat, flat, ALU.mult).then_inc(s.sq_done, 1)
        dve.wait_ge(s.sq_done, t + 1)
        sq = m.squares[:, :].rearrange("p (a k m) -> p a k m", k=2, m=N)
        mag2, mag = (x[:, :].rearrange("p (a m) -> p a m", m=N) for x in (m.mag2, m.mag))
        nc.vector.scalar_tensor_tensor(out=mag2, in0=sq[:, :, 0, :], scalar=1e-8, in1=sq[:, :, 1, :],
                                       op0=ALU.add, op1=ALU.add).then_inc(s.mag2_done, 1)
        dve.wait_ge(s.mag_done, t + 1)
        nc.vector.tensor_reduce(m.top[:, :], mag, AX.X, ALU.max).then_inc(s.max_done, 1)
        dve.wait_ge(s.max_done, t + 1)
        nc.vector.tensor_tensor(mag, mag, m.top[:, :, None].to_broadcast([P, 32, N]), ALU.subtract).then_inc(s.shifted, 1)
        dve.wait_ge(s.exp_done, t + 1)
        nc.vector.tensor_reduce(m.total[:, :], mag2, AX.X, ALU.add).then_inc(s.total_done, 1)
        dve.wait_ge(s.total_done, t + 1)
        nc.vector.reciprocal(m.inverse[:, :], m.total[:, :]).then_inc(s.inverse_done, 1)
        dve.wait_ge(s.inverse_done, t + 1)
        nc.vector.tensor_tensor(m.weights[:, bass.ts(t, P)].rearrange("p (a m) -> p a m", m=N), mag2,
                                m.inverse[:, :, None].to_broadcast([P, 32, N]), ALU.mult).then_inc(s.softmaxed, 1)

    lo(0, 0)

    def step(i, k, more):
        if more:
            lo(*following(i, k, 8))
        take_scores(i, k)
        if k % PAIRS == PAIRS - 1:
            softmax(i, k)

    rolled(dve, STEPS_Q // 8, 8, step, 1)



LATE_PAIR = X_UNITS // 2 + HALVES * (PER_HALF + X_UNITS // 2)


def matrix_slot(m, mat, k):
    return [m.x[:, part, bass.ts(2 * mat + k, UNIT)] for part in range(2)]


def matrix(m, mat, c, cols):
    return [m.x[:, part, mat * C * D + c * D:mat * C * D + (c + 1) * D][:, cols] for part in range(2)]


def load_matrix(sp, io, m, s, index):
    q = LATE_PAIR + index
    for k in range(2):
        sp.wait_ge(s.lo_done, q * 2 + (k - 1))
        sp.dma_start(m.raw[:, k, :], io.late_units[index * 2 + k]).then_inc(s.raw_loaded[k], 16)


def values_sync(nc, sp, io, m, s):
    for index in range(4):
        load_matrix(sp, io, m, s, index)
        if index == 0:
            sp.wait_ge(s.projected, 4 * STEPS_Q)
            load_tile(sp, m, io.s_scr, 0, 0, s.v_tile_loaded)
    with sp.Fori(1, TILES) as t:
        sp.wait_ge(s.gathered, t * 4)
        load_tile(sp, m, io.s_scr, 0, t, s.v_tile_loaded)


def values_tensor(nc, pe, io, m, s):
    grouped = m.h[:, 1, :].rearrange("p (g a b c w) -> p g a b c w", g=GROUPS, a=2, b=2, c=C)

    def value(t, g):
        pe.wait_ge(s.gathered, t * 4 + (g + 1))
        for ri in range(2):
            if g or not isinstance(t, int) or t:
                pe.wait_ge(s.v_lo, t * 8 + (2 * g + ri - 1))
            else:
                pe.wait_ge(s.lo_done, 2 * (LATE_PAIR + ri + 1))
            for c in range(C):
                st = [grouped[:, g, ri, part, c, :] for part in range(2)]
                last = product(nc, m.stat[:, ri, :], st, matrix(m, ri, c, slice(0, D)), c == 0, c == C - 1)
            last.then_inc(s.v_done, 1)

    def turn(t):
        pe.wait_ge(s.spread_done, t + 1)
        if not isinstance(t, int) or t:
            pe.wait_ge(s.at_lo, t * 8 - 8)
        for a in range(N):
            last = nc.tensor.matmul(m.stat[:, 2, 0:P], m.select[:, a, :], m.spread[:, a, :],
                                    start=a == 0, stop=a == N - 1)
        last.then_inc(s.wt_done, 1)

    def weigh(t, g):
        pe.wait_ge(s.v_lo, t * 8 + (2 * g + 2))
        pe.wait_ge(s.wf_hi, t * 4 + (g + 1))
        pe.wait_ge(s.wf_lo, t * 4 + (g + 1))
        for ri in range(2):
            if g or not isinstance(t, int) or t:
                pe.wait_ge(s.ot_lo, t * 16 + (4 * g + 2 * ri - 2))
            for j in range(PAIRS):
                st = [m.v[:, g % 2, ri, part, bass.ts(j, P)] for part in range(2)]
                mv = [m.wf[:, part, bass.ts(j, 2 * P)] for part in range(2)]
                last = product(nc, m.acc[:, 2 * ri + j // 2, bass.ts(j % 2, 2 * P)], st, mv, True, True)
            last.then_inc(s.weighed, 1)

    def project(t, more):
        if more:
            pe.wait_ge(s.wt_lo, t + 2)
        for e in range(2 * C):
            ri, ec = divmod(e, C)
            if ec == 0:
                pe.wait_ge(s.ot_lo, t * 16 + (14 + 2 * ri))
            if e or not isinstance(t, int) or t:
                if e >= 2 or not isinstance(t, int) or t:
                    pe.wait_ge(s.at_lo, t * 8 + (e - 1))
            for j in range(PAIRS):
                last = product(nc, m.stat[:, 2 + e % 2, :], matrix(m, 2 + ri, j, bass.ts(ec, P)),
                               [m.ot[:, ri, part, j, :] for part in range(2)], j == 0, j == PAIRS - 1)
            last.then_inc(s.attn_done, 1)

    pe.wait_ge(s.compacted, 4 * STEPS_Q)
    value(0, 0)
    turn(0)
    def project_bias():
        pe.wait_ge(s.lo_done, 2 * (LATE_PAIR + 4))
        pe.wait_ge(s.bv_done, 2)
        for e in range(2 * C):
            ri, ec = divmod(e, C)
            for j in range(PAIRS):
                for part in range(2):
                    last = nc.tensor.matmul(m.stat[:, 3, 2 * e:2 * e + 2], matrix(m, 2 + ri, j, bass.ts(ec, P))[part],
                                            m.bv[:, ri, j, :], start=j == 0 and part == 0, stop=j == PAIRS - 1 and part == 1)
        last.then_inc(s.bias_done, 1)

    def tile(t, _, more):
        for g in range(GROUPS):
            if g + 1 < GROUPS:
                value(t, g + 1)
            elif more:
                value(t + 1, 0)
                turn(t + 1)
            weigh(t, g)
        if isinstance(t, int) and t == 0:
            project_bias()
            pe.wait_ge(s.bo_done, 1)
        project(t, more)

    rolled(pe, TILES, 1, tile, 1)


def values_scalar(nc, act, io, m, s):
    act.wait_ge(s.projected, 4 * STEPS_Q)
    def v_hi(t, g):
        if g >= 2 or not isinstance(t, int) or t:
            act.wait_ge(s.weighed, t * 8 + (2 * g - 2))
        for ri in range(2):
            act.wait_ge(s.v_done, t * 8 + (2 * g + ri + 1))
            nc.scalar.copy(m.v[:, g % 2, ri, 0, :], m.stat[:, ri, :]).then_inc(s.v_hi, 1)

    def wt_hi(t):
        act.wait_ge(s.wt_done, t + 1)
        if not isinstance(t, int) or t:
            act.wait_ge(s.wf_hi, t * 4)
            act.wait_ge(s.wf_lo, t * 4)
        nc.scalar.copy(m.wt[:, 0, :], m.stat[:, 2, 0:P]).then_inc(s.wt_hi, 1)

    def ot_hi(t, g):
        if g == 0 and (not isinstance(t, int) or t):
            act.wait_ge(s.attn_done, t * 8)
        for ri in range(2):
            act.wait_ge(s.weighed, t * 8 + (2 * g + ri + 1))
            for hh in range(2):
                out, src = head_blocks(m, ri, hh, g)
                nc.scalar.copy(out[0], src).then_inc(s.ot_hi, 1)

    def at_hi(t):
        if isinstance(t, int) and t == 0:
            act.wait_ge(s.bo_done, 2)
        for e in range(2 * C):
            act.wait_ge(s.attn_done, t * 8 + (e + 1))
            if e >= 2 or not isinstance(t, int) or t:
                act.wait_ge(s.at_stored[e % 2], t * 128 + 32 * (e // 2))
            nc.scalar.activation(stage(m, e)[0].bitcast(F32R), m.stat[:, 2 + e % 2, :], ACT.Identity,
                                 bias=m.bo[:, e:e + 1]).then_inc(s.at_hi, 1)

    def cut(mat):
        for k in range(2):
            cut_hi(nc, act, m, s, LATE_PAIR + mat, matrix_slot(m, mat, k), k)

    cut(0)
    cut(1)
    act.wait_ge(s.scored, 4 * STEPS_Q)
    act.wait_ge(s.softmaxed, TILES)
    at = PARAM["v_r"]
    nc.scalar.copy(m.bv[:, :, :, 0].rearrange("p a b -> p (a b)"), m.params[:, at:at + 8]).then_inc(s.bv_done, 1)
    v_hi(0, 0)
    wt_hi(0)
    cut(2)
    cut(3)

    def tile(t, _, more):
        for g in range(GROUPS):
            if g + 1 < GROUPS:
                v_hi(t, g + 1)
            elif more:
                v_hi(t + 1, 0)
                wt_hi(t + 1)
            ot_hi(t, g)
        at_hi(t)

    rolled(act, TILES, 1, tile, 1)


def head_blocks(m, ri, hh, g):
    part = slice(64 * hh, 64 * hh + 64)
    out = [m.ot[part, ri, half, :, :].rearrange("p j (n r) -> p j n r", n=N)[:, :, :, 32 * g:32 * g + 32] for half in range(2)]
    src = m.acc[part, 2 * ri:2 * ri + 2, :].rearrange("p b (j h n r) -> p (b j) h n r", j=2, h=2, n=N)[:, :, hh, :, :]
    return out, src


def stage(m, e):
    return m.raw[:, e % 2, 0:512], m.raw[:, e % 2, 512:1024]


def values_vector(nc, dve, io, m, s):
    tiles = m.h[:, 0, :].rearrange("p (q g r) -> p q g r", g=GROUPS, r=32)
    grouped = m.h[:, 1, :].rearrange("p (g q r) -> p g q r", g=GROUPS, r=32)

    def gather(t, g):
        dve.wait_ge(s.v_tile_loaded, t * (16 * TILE_DMAS) + 16 * TILE_DMAS)
        if not isinstance(t, int) or t:
            dve.wait_ge(s.v_done, t * 8 + (2 * g - 6))
        nc.vector.tensor_copy(grouped[:, g], tiles[:, :, g, :].bitcast(F32)).then_inc(s.gathered, 1)

    def spread(t):
        if not isinstance(t, int) or t:
            dve.wait_ge(s.wt_done, t)
        w = m.weights[:, bass.ts(t, P)].rearrange("p (h m) -> p m h", m=N)
        nc.vector.tensor_tensor(m.spread[:, :, :].rearrange("p m (h n) -> p m h n", n=N),
                                w[:, :, :, None].to_broadcast([P, N, 32, N]),
                                m.own_n[:, None, None, :].to_broadcast([P, N, 32, N]), ALU.mult).then_inc(s.spread_done, 1)

    def v_lo(t, g):
        for ri in range(2):
            dve.wait_ge(s.v_hi, t * 8 + (2 * g + ri + 1))
            nc.vector.tensor_tensor(m.v[:, g % 2, ri, 1, :], m.stat[:, ri, :], m.v[:, g % 2, ri, 0, :].bitcast(F32),
                                    ALU.subtract).then_inc(s.v_lo, 1)

    def wt_lo(t):
        dve.wait_ge(s.wt_hi, t + 1)
        nc.vector.tensor_tensor(m.wt[:, 1, :], m.stat[:, 2, 0:P], m.wt[:, 0, :].bitcast(F32), ALU.subtract).then_inc(s.wt_lo, 1)

    def ot_lo(t, g):
        for ri in range(2):
            for hh in range(2):
                out, src = head_blocks(m, ri, hh, g)
                dve.wait_ge(s.ot_hi, t * 16 + (4 * g + 2 * ri + hh + 1))
                nc.vector.tensor_tensor(out[1], src, out[0].bitcast(F32), ALU.subtract).then_inc(s.ot_lo, 1)

    def at_lo(t):
        for e in range(2 * C):
            dve.wait_ge(s.at_hi, t * 8 + (e + 1))
            nc.vector.scalar_tensor_tensor(out=stage(m, e)[1].bitcast(F32R), in0=m.stat[:, 2 + e % 2, :],
                                           scalar=m.bo[:, e:e + 1], in1=stage(m, e)[0],
                                           op0=ALU.add, op1=ALU.subtract).then_inc(s.at_lo, 1)

    def cut(mat):
        for k in range(2):
            cut_lo(nc, dve, m, s, LATE_PAIR + mat, matrix_slot(m, mat, k), k)

    def output_bias():
        dve.wait_ge(s.bias_done, 1)
        nc.vector.tensor_reduce(m.bo[:, :], m.stat[:, 3, 0:16].rearrange("p (e k) -> p e k", k=2), AX.X, ALU.add).then_inc(s.bo_done, 1)
        dve.wait_ge(s.bo_done, 1)
        at = PARAM["o_r"]
        nc.vector.tensor_tensor(m.bo[:, :], m.bo[:, :], m.params[:, at:at + 8], ALU.add).then_inc(s.bo_done, 1)

    cut(0)
    gather(0, 0)
    cut(1)
    dve.wait_ge(s.scored, 4 * STEPS_Q)
    dve.wait_ge(s.softmaxed, TILES)
    spread(0)
    v_lo(0, 0)
    wt_lo(0)
    expand(nc, nc.vector, dve, m, s, 0, 0, 0)
    for g in range(1, GROUPS):
        gather(0, g)
    at = PARAM["v_r"]
    dve.wait_ge(s.bv_done, 1)
    nc.vector.tensor_tensor(m.bv[:, :, :, 1].rearrange("p a b -> p (a b)"), m.params[:, at:at + 8],
                            m.bv[:, :, :, 0].rearrange("p a b -> p (a b)").bitcast(F32), ALU.subtract).then_inc(s.bv_done, 1)
    cut(2)
    cut(3)

    def tile(t, _, more):
        for g in range(GROUPS):
            if g + 1 < GROUPS:
                v_lo(t, g + 1)
            elif more:
                v_lo(t + 1, 0)
            if g == 1 and more:
                spread(t + 1)
            if g >= 2 and more:
                for other in (2 * g - 4, 2 * g - 3):
                    gather(t + 1, other)
            if g == 3 and more:
                wt_lo(t + 1)
            ot_lo(t, g)
            if g + 1 < GROUPS:
                expand(nc, nc.vector, dve, m, s, t, g + 1, 0)
            elif more:
                expand(nc, nc.vector, dve, m, s, t + 1, 0, 0)
        if isinstance(t, int) and t == 0:
            output_bias()
        at_lo(t)

    rolled(dve, TILES, 1, tile, 1)


def expand(nc, engine, queue, m, s, t, g, part):
    queue.wait_ge(s.wt_lo if part else s.wt_hi, t + 1)
    if g or not isinstance(t, int) or t:
        queue.wait_ge(s.weighed, t * 8 + 2 * g)
    w = m.wt[:, part, :].bitcast(F32).rearrange("p (h g n) -> p h g n", g=GROUPS, n=N)[:, :, g, :]
    engine.tensor_tensor(m.wf[:, part, :].rearrange("p (h n r) -> p h n r", n=N, r=32),
                         w[:, :, :, None].to_broadcast([P, HEADS, N, 32]),
                         m.own_row[:, None, None, :].to_broadcast([P, HEADS, N, 32]),
                         ALU.mult).then_inc(s.wf_lo if part else s.wf_hi, 1)


def values_pool(nc, pool, io, m, s):
    pool.wait_ge(s.scored, 4 * STEPS_Q)
    pool.wait_ge(s.softmaxed, TILES)

    expand(nc, nc.gpsimd, pool, m, s, 0, 0, 1)

    def tile(t, _, more):
        for g in range(1, GROUPS):
            expand(nc, nc.gpsimd, pool, m, s, t, g, 1)
        for e in range(2 * C):
            if e == C and more:
                expand(nc, nc.gpsimd, pool, m, s, t + 1, 0, 1)
            ri, ec = divmod(e, C)
            pool.wait_ge(s.at_lo, t * 8 + (e + 1))
            for part in range(2):
                pool.dma_start(io.a_scr[ri, part, :, ec, :, bass.ts(t, P)].rearrange("n p r -> p n r"),
                               stage(m, e)[part].rearrange("p (n r) -> p n r", n=N)).then_inc(s.at_stored[e % 2], 16)

    rolled(pool, TILES, 1, tile, 1)



ROWS = 4
I_STEPS = HALVES * N
I_TILES = I_STEPS * ROWS
W = D // 2
PAIRS_OF_N = [(0, 1), (0, 2), (0, 3), (1, 2), (1, 3), (2, 3)]
TINY = 2.0 ** -120
M_FIRST = 4 + 2 * N
LATE_ORDER = list(range(4)) + list(range(4, 4 + 2 * N)) * HALVES + [M_FIRST + k for k in range(5)]


def bank(m, b):
    return m.acc[:, b, :] if b < 4 else m.stat[:, b - 4, :]


def quarter(m, q):
    return m.h[:, 0, q * 4096:(q + 1) * 4096].rearrange("p (a b c r) -> p a b c r", a=2, b=2, c=C)


def sup_view(m):
    return m.h[:, 1, :].rearrange("p (b a c r) -> p b a c r", a=2, b=2, c=C)


def piece(buffer, y):
    return buffer[:, y % 2, :].rearrange("p (n k d) -> p n k d", n=N, k=2)


def squared(m, y):
    return m.n2[:, y % 2, :].rearrange("p (n d) -> p n d", n=N)


def cosine(m, y, i, j):
    n = PAIRS_OF_N.index((min(i, j), max(i, j)))
    sq = piece(m.sq, y)
    return sq[:, n, 0, :] if n < 4 else sq[:, 2 * (n - 4), 1, :]


def zero_sums(m, y):
    return m.n2[:, y % 2, W:N * W].bitcast(BF16).rearrange("p (a d) -> p a d", d=W)


def strength(m, x, i, j):
    return m.strength[:, x, N * i + j:N * i + j + 1]


def load_stream(sp, io, m, s, at, units=2):
    for k in range(units):
        sp.wait_ge(s.lo_done, (LATE_PAIR + at) * 2 + k - 1)
        sp.dma_start(m.raw[:, k, :], io.late_units[LATE_ORDER[at] * 2 + k]).then_inc(s.raw_loaded[k], 16)


def final_sync(nc, sp, io, m, s):
    def load_quarter(step, q):
        half, n = divmod(step, N)
        a = step * 2 + q
        if a >= 2:
            sp.wait_ge(s.i_done, 2 * (a - 1))
        rows = half * HALF + q * 256
        for ri in range(2):
            for part in range(2):
                sp.dma_start(quarter(m, q)[:, ri, part].bitcast(F32),
                             io.a_scr[ri, part, n, :, :, rows:rows + 256].rearrange("c p r -> p c r")
                             ).then_inc(s.quarter_loaded[q], 16)

    for e in range(2):
        sp.wait_ge(s.at_stored[e], 128 * TILES)
    load_stream(sp, io, m, s, 4)
    load_quarter(0, 0)
    load_stream(sp, io, m, s, 5)
    load_quarter(0, 1)
    for mat in range(2):
        load_stream(sp, io, m, s, 6 + mat)
    for step in range(1, I_STEPS):
        for q in range(2):
            load_quarter(step, q)
        for mat in range(2):
            load_stream(sp, io, m, s, 6 + 2 * step + mat)
    for mat in range(2):
        load_stream(sp, io, m, s, 22 + mat)
    load_stream(sp, io, m, s, 24, 1)


def final_tensor(nc, pe, io, m, s):
    def interfere(step):
        for q in range(2):
            pe.wait_ge(s.quarter_loaded[q], 64 * (step + 1))
            for tk in range(2):
                k = (step * 2 + q) * 2 + tk
                if k >= 2:
                    pe.wait_ge(s.r_done, k - 1)
                    pe.wait_ge(s.i_out, k - 1)
                for out, parts in enumerate((((0, 0),), ((1, 1),), ((0, 1), (1, 0)))):
                    if k % 4 == 0 and out < 2:
                        pe.wait_ge(s.lo_done, (LATE_PAIR + 5 + 2 * step + out) * 2)
                    for x, (ri, mat) in enumerate(parts):
                        for c in range(C):
                            st = [quarter(m, q)[:, ri, part, c, bass.ts(tk, P)] for part in range(2)]
                            last = product(nc, bank(m, 3 * (k % 2) + out), st,
                                           matrix(m, 2 * (step % 2) + mat, c, slice(0, D)),
                                           x == 0 and c == 0, x == len(parts) - 1 and c == C - 1)
                last.then_inc(s.i_done, 1)
                if step > N and k % 4 == 1:
                    turn(step - N - 1)

    def turn(x):
        pe.wait_ge(s.sup_done, x + 1)
        if x:
            pe.wait_ge(s.sup_lo, 2 * x)
        for ri in range(2):
            for c in range(C):
                last = nc.tensor.transpose(bank(m, 6 + ri)[:, bass.ts(c, P)], m.sup[:, ri, bass.ts(c, P)],
                                           m.table[:, :])
            last.then_inc(s.turned, 1)

    def measure(h):
        pe.wait_ge(s.sup_lo, 8 * (h + 1))
        if h:
            pe.wait_ge(s.y_out, h)
        for e in range(C):
            u = h * C + e
            if e >= 2:
                pe.wait_ge(s.mr_done, u - 1)
                pe.wait_ge(s.mi_sq, u - 1)
            for out, parts in enumerate((((0, 0),), ((1, 1),), ((1, 0), (0, 1)))):
                for x, (mat, ri) in enumerate(parts):
                    for c in range(C):
                        mv = [sup_view(m)[:, part, ri, c, :] for part in range(2)]
                        last = product(nc, bank(m, 3 * (e % 2) + out), matrix(m, mat, c, bass.ts(e, P)), mv,
                                       x == 0 and c == 0, x == len(parts) - 1 and c == C - 1)
            last.then_inc(s.measured, 1)

    def post(h):
        pe.wait_ge(s.amp_lo, C * (h + 1))
        for e in range(C):
            u = h * C + e
            if e >= 2:
                pe.wait_ge(s.z_sq, u - 1)
            for c in range(C):
                mv = [m.a[:, part, bass.ts(c, HALF)] for part in range(2)]
                last = product(nc, bank(m, e % 2), matrix(m, 2, c, bass.ts(e, P)), mv, c == 0, c == C - 1)
            last.then_inc(s.posted, 1)
        pe.wait_ge(s.z_sums, 2 * (h + 1))
        pe.wait_ge(s.mean_ready, h + 1)
        for k in range(2):
            last = nc.tensor.matmul(bank(m, 4 + k), m.mean_of_out.bitcast(F32), m.pair[:, k, :], start=True, stop=True)
        last.then_inc(s.z_means, 1)

    def top(h):
        pe.wait_ge(s.z_lo, C * (h + 1))
        for j in range(C + 1):
            u = h * C + j
            if j < C:
                if j >= 2:
                    pe.wait_ge(s.top_sum, u - 1)
                for c in range(C):
                    mv = [m.a[:, part, bass.ts(c, HALF)] for part in range(2)]
                    last = product(nc, bank(m, j % 2), matrix(m, 3, c, bass.ts(j, P)), mv, c == 0, c == C - 1)
                last.then_inc(s.topped, 1)
            if j:
                pe.wait_ge(s.h1_lo, u)
                for k in range(2):
                    st = [m.top2[:, part, (j - 1) * 256 + k * P:(j - 1) * 256 + (k + 1) * P] for part in range(2)]
                    mv = [m.h1[:, (j - 1) % 2, part, :] for part in range(2)]
                    last = product(nc, bank(m, 2 + k), st, mv, j == 1, j == C)
                last.then_inc(s.h2_part, 1)
        pe.wait_ge(s.h2_done, 2 * (h + 1))
        for k in range(2):
            last = nc.tensor.matmul(bank(m, 4)[0:1, :], act_bias(m.params, "w3", k), m.pair[:, k, :],
                                    start=k == 0, stop=k == 1)
        last.then_inc(s.y_done, 1)

    pe.wait_ge(s.at_lo, 2 * C * TILES)
    for step in range(I_STEPS):
        interfere(step)
    turn(3)
    pe.wait_ge(s.lo_done, (LATE_PAIR + 24) * 2 + 1)
    for x, part in ((4, measure), (5, post), (6, top)):
        part(0)
        turn(x)
    turn(7)
    for part in (measure, post, top):
        part(1)


def final_scalar(nc, act, io, m, s):
    def cut(at, mat, units=2):
        for k in range(units):
            dst = matrix_slot(m, mat, k) if mat < 4 else [m.top2[:, part, :] for part in range(2)]
            cut_hi(nc, act, m, s, LATE_PAIR + at, dst, k)

    def take(step, k4):
        k = step * 4 + k4
        b = 3 * (k % 2)
        act.wait_ge(s.i_done, k + 1)
        if k >= 2:
            act.wait_ge(s.ri_stored[k % 2], 16 * (k // 2))
        nc.scalar.copy(m.stage[:, k % 2, 0:512], bank(m, b + 1)).then_inc(s.aiwi_out, 1)
        nc.scalar.copy(m.stage[:, k % 2, 512:1024], bank(m, b + 2)).then_inc(s.i_out, 1)

    def squares(y):
        act.wait_ge(s.ri_loaded[y % 2], 16 * (y // 2 + 1))
        if y >= 2:
            act.wait_ge(s.f_done, 8 * (y - 1))
            act.wait_ge(s.f_first, 4 * (y - 1))
        nc.scalar.activation(m.sq[:, y % 2, :], m.ri[:, y % 2, :], ACT.Square).then_inc(s.x_sq, 1)

    def guess(y):
        g = m.sq[:, y % 2, 0:N * W]
        act.wait_ge(s.x_sum, y + 1)
        nc.scalar.activation(g, m.n2[:, y % 2, :], ACT.Ln, bias=act_bias(m.params, "tiny", 0)).then_inc(s.x_ln, 1)
        act.wait_ge(s.x_ln, y + 1)
        nc.scalar.activation(g, g, ACT.Exp, scale=-0.5).then_inc(s.x_guess, 1)
        act.wait_ge(s.x_guess, y + 1)
        nc.scalar.activation(m.sq[:, y % 2, N * W:], g, ACT.Square).then_inc(s.x_guess_sq, 1)

    def first_terms(y):
        for j in range(N):
            if j == 0:
                act.wait_ge(s.cos_done, 2 * y + 1)
            if j == N - 1:
                act.wait_ge(s.cos_done, 2 * y + 2)
            i = 1 if j == 0 else 0
            nc.scalar.activation(m.n2[:, y % 2, bass.ts(j, W)], cosine(m, y, i, j), ACT.Identity,
                                 bias=strength(m, y // 2, j, j), scale=strength(m, y // 2, i, j)).then_inc(s.f_first, 1)

    def norm(x):
        act.wait_ge(s.sup_sum, 2 * x + 2)
        sup = m.sup[:, :, :].rearrange("p k d -> p (k d)")
        nc.scalar.activation(m.u[:, 1, N * W:], sup, ACT.Square, accum_out=m.norms[:, 0:1]).then_inc(s.norm_sum, 1)
        act.wait_ge(s.norm_sum, x + 1)
        nc.scalar.activation(m.norms[:, 1:2], m.norms[:, 0:1], ACT.Sqrt, bias=act_bias(m.params, "norm_eps", 0)).then_inc(s.norm_root, 1)
        act.wait_ge(s.norm_inverse, x + 1)
        nc.scalar.activation(sup, sup, ACT.Identity, scale=m.norms[:, 2:3]).then_inc(s.sup_done, 1)

    def sup_hi(x):
        h, r = divmod(x, ROWS)
        if h and r == 0:
            act.wait_ge(s.measured, C)
        for ri in range(2):
            act.wait_ge(s.turned, 2 * x + ri + 1)
            nc.scalar.copy(sup_view(m)[:, 0, ri, :, bass.ts(r, P)],
                           bank(m, 6 + ri).rearrange("p (c r) -> p c r", r=P)).then_inc(s.sup_hi, 1)

    def measure(h, e):
        u = h * C + e
        act.wait_ge(s.measured, u + 1)
        if u % C == 0 and h:
            act.wait_ge(s.y_done, h)
        nc.scalar.copy(m.pair[:, 0, :], bank(m, 3 * (e % 2) + 1)).then_inc(s.misi_out, 1)
        nc.scalar.activation(m.pair[:, 1, :], bank(m, 3 * (e % 2) + 2), ACT.Square).then_inc(s.mi_sq, 1)
        act.wait_ge(s.amp_sq, u + 1)
        nc.scalar.activation(m.pair[:, 0, :], m.pair[:, 0, :], ACT.Sqrt).then_inc(s.amp_root, 1)
        act.wait_ge(s.amp_root, u + 1)
        nc.scalar.copy(m.a[:, 0, bass.ts(e, HALF)], m.pair[:, 0, :]).then_inc(s.amp_hi, 1)
        act.wait_ge(s.amp_lo, u + 1)

    def post(h, k):
        z = m.raw.rearrange("p a w -> p (a w)")
        if k == 0:
            act.wait_ge(s.lo_done, (LATE_PAIR + 24) * 2 + 1)
            if h:
                act.wait_ge(s.z_lo, C * h)
        for e in range(2 * k, 2 * k + 2) if k < 2 else ():
            u = h * C + e
            cols = bass.ts(e, HALF)
            act.wait_ge(s.posted, u + 1)
            if e:
                act.wait_ge(s.z_sq_added, u)
            bias = act_bias(m.params, "post_b", e)
            nc.scalar.activation(z[:, cols], bank(m, e % 2), ACT.Identity, bias=bias).then_inc(s.z_pre, 1)
            nc.scalar.activation(m.pair[:, 0, :], bank(m, e % 2), ACT.Square, bias=bias).then_inc(s.z_sq, 1)
        if k == 2:
            act.wait_ge(s.z_means, h + 1)
            nc.scalar.activation(m.pair[:, 0, :], bank(m, 4), ACT.Square).then_inc(s.z_mean_sq, 1)
            act.wait_ge(s.z_var, h + 1)
            nc.scalar.activation(m.pair[:, 0, :], m.pair[:, 1, :], ACT.Sqrt).then_inc(s.z_std, 1)
        for e in range(C) if k == 3 else ():
            u = h * C + e
            cols = bass.ts(e, HALF)
            act.wait_ge(s.z_scaled, u + 1)
            nc.scalar.activation(z[:, cols], z[:, cols], ACT.Gelu, bias=act_bias(m.params, "post_be", e),
                                 scale=act_bias(m.params, "post_g", e)).then_inc(s.z_gelu, 1)
            act.wait_ge(s.z_gelu, u + 1)
            nc.scalar.copy(m.a[:, 0, cols], z[:, cols]).then_inc(s.z_hi, 1)

    def top(h, j):
        u = h * C + j
        act.wait_ge(s.top_sum, u + 1)
        if u >= 2:
            act.wait_ge(s.h2_part, u - 1)
        nc.scalar.activation(m.h1[:, j % 2, 0, :], m.top_x[:, j % 2, :], ACT.Relu).then_inc(s.h1_hi, 1)
        if j < C - 1:
            return
        act.wait_ge(s.h2_part, C * (h + 1))
        for k in range(2):
            nc.scalar.activation(m.pair[:, k, :], bank(m, 2 + k), ACT.Relu,
                                 bias=act_bias(m.params, "top2", k)).then_inc(s.h2_done, 1)
        act.wait_ge(s.y_done, h + 1)
        nc.scalar.copy(m.top_x[0:1, 0, :], bank(m, 4)[0:1, :]).then_inc(s.y_out, 1)
        act.wait_ge(s.y_out, h + 1)
        act.dma_start(io.y[h:h + 1, :], m.top_x[0:1, 0, :]).then_inc(s.y_stored, 16)

    def following_pieces(x, more):
        if more:
            squares(2 * x + 2)
        first_terms(2 * x + 1)
        if more:
            guess(2 * x + 2)

    def tile(x, part):
        if x > ROWS:
            norm(x - 1)
        part(0, 0)
        squares(2 * x + 1)
        first_terms(2 * x)
        guess(2 * x + 1)
        part(0, 1)
        if x > ROWS:
            sup_hi(x - 1)
        part(0, 2)
        following_pieces(x, x + 1 < TILES)
        part(0, 3)

    def nothing(h, k):
        pass

    act.wait_ge(s.attn_done, 2 * C * TILES)
    act.wait_ge(s.at_lo, 2 * C * TILES)
    for mat in range(4):
        cut(4 + mat, mat)
    for step in range(I_STEPS):
        x = step - N
        if x == 0:
            squares(0)
            guess(0)
        take(step, 0)
        if x > 0:
            norm(x - 1)
        take(step, 1)
        if step:
            cut(6 + 2 * step, 2 * ((step + 1) % 2))
        if x >= 0:
            squares(2 * x + 1)
            first_terms(2 * x)
            guess(2 * x + 1)
        if step:
            cut(7 + 2 * step, 2 * ((step + 1) % 2) + 1)
        take(step, 2)
        if x > 0:
            sup_hi(x - 1)
        take(step, 3)
        if x >= 0:
            following_pieces(x, step + 1 < I_STEPS)
    norm(3)
    for mat in range(2):
        cut(22 + mat, 2 + mat)
    sup_hi(3)
    act.wait_ge(s.ri_stored[0], 16 * I_TILES // 2)
    act.wait_ge(s.ri_stored[1], 16 * I_TILES // 2)
    act.wait_ge(s.r_done, I_TILES)
    cut(24, 4, 1)
    squares(2 * ROWS)
    guess(2 * ROWS)
    for x, part in ((4, measure), (5, post), (6, top), (7, nothing)):
        tile(x, part)
    norm(7)
    sup_hi(7)
    for part in (measure, post, top):
        for k in range(4):
            part(1, k)
    act.wait_ge(s.y_stored, 32)


def final_vector(nc, dve, io, m, s):
    def cut(at, mat, units=2):
        for k in range(units):
            dst = matrix_slot(m, mat, k) if mat < 4 else [m.top2[:, part, :] for part in range(2)]
            cut_lo(nc, dve, m, s, LATE_PAIR + at, dst, k)

    def take(step, k4):
        k = step * 4 + k4
        dve.wait_ge(s.aiwi_out, k + 1)
        real = m.stage[:, k % 2, 0:512]
        nc.vector.tensor_tensor(real, bank(m, 3 * (k % 2)), real, ALU.subtract).then_inc(s.r_done, 1)

    def directions(y):
        sq = piece(m.sq, y)
        dve.wait_ge(s.x_sq, y + 1)
        nc.vector.tensor_tensor(squared(m, y), sq[:, :, 0, :], sq[:, :, 1, :], ALU.add).then_inc(s.x_sum, 1)

    def units(y):
        guess, step = m.sq[:, y % 2, 0:N * W], m.sq[:, y % 2, N * W:]
        dve.wait_ge(s.x_guess_sq, y + 1)
        nc.vector.scalar_tensor_tensor(out=step, in0=step, scalar=-0.5, in1=m.n2[:, y % 2, :], op0=ALU.mult,
                                       op1=ALU.mult).then_inc(s.x_step, 1)
        dve.wait_ge(s.x_step, y + 1)
        nc.vector.scalar_tensor_tensor(out=guess, in0=step, scalar=1.5, in1=guess, op0=ALU.add, op1=ALU.mult).then_inc(s.x_inverse, 1)
        dve.wait_ge(s.x_inverse, y + 1)
        if y >= 2:
            dve.wait_ge(s.sup_sum, y - 1)
        inverse = guess.rearrange("p (n d) -> p n d", n=N)
        nc.vector.tensor_tensor(piece(m.u, y), piece(m.ri, y), inverse[:, :, None, :].to_broadcast([P, N, 2, W]),
                                ALU.mult).then_inc(s.u_done, 1)
        dve.wait_ge(s.u_done, y + 1)

    def cosines(y):
        zp, sq, u = zero_sums(m, y), piece(m.sq, y), piece(m.u, y)
        for n, (i, j) in enumerate(PAIRS_OF_N[:4]):
            nc.vector.tensor_tensor(sq[:, n], u[:, i], u[:, j], ALU.mult).then_inc(s.pair_mul, 1)
        dve.wait_ge(s.pair_mul, 6 * y + 4)
        nc.vector.tensor_tensor(sq[:, :, 0, :], sq[:, :, 0, :], sq[:, :, 1, :], ALU.add).then_inc(s.pair_sum, 1)
        dve.wait_ge(s.pair_sum, 3 * y + 1)
        dve.wait_ge(s.zero_pairs, 6 * y + 6)
        nc.vector.tensor_tensor(sq[:, :, 0, :], sq[:, :, 0, :], zp[:, 0:4, :], ALU.add).then_inc(s.cos_done, 1)

    def last_cosines(y):
        zp, sq, u = zero_sums(m, y), piece(m.sq, y), piece(m.u, y)
        for n, (i, j) in enumerate(PAIRS_OF_N[4:]):
            nc.vector.tensor_tensor(sq[:, 2 * n:2 * n + 2, 1, :], u[:, i], u[:, j], ALU.mult).then_inc(s.pair_mul, 1)
        for n in range(2):
            dve.wait_ge(s.pair_mul, 6 * y + 5 + n)
            nc.vector.tensor_tensor(sq[:, 2 * n, 1, :], sq[:, 2 * n, 1, :], sq[:, 2 * n + 1, 1, :], ALU.add).then_inc(s.pair_sum, 1)
        dve.wait_ge(s.pair_sum, 3 * y + 3)
        nc.vector.tensor_tensor(sq[:, 0:4:2, 1, :], sq[:, 0:4:2, 1, :], zp[:, 4:6, :], ALU.add).then_inc(s.cos_done, 1)
        dve.wait_ge(s.cos_done, 2 * y + 2)

    def superpose(y):
        f = squared(m, y)
        for n in range(1, 3):
            for j in range(N):
                i = [k for k in range(N) if k != j][n]
                if n == 1:
                    dve.wait_ge(s.f_first, 4 * y + j + 1)
                else:
                    dve.wait_ge(s.f_done, 8 * y + j + 1)
                nc.vector.scalar_tensor_tensor(out=f[:, j], in0=cosine(m, y, i, j), scalar=strength(m, y // 2, i, j), in1=f[:, j],
                                               op0=ALU.mult, op1=ALU.add).then_inc(s.f_done, 1)
        dve.wait_ge(s.f_done, 8 * y + 8)
        nc.vector.tensor_tensor(piece(m.u, y), piece(m.ri, y), f[:, :, None, :].to_broadcast([P, N, 2, W]),
                                ALU.mult).then_inc(s.fz_done, 1)

    def invert_norm(x):
        dve.wait_ge(s.norm_root, x + 1)
        nc.vector.reciprocal(m.norms[:, 2:3], m.norms[:, 1:2]).then_inc(s.norm_inverse, 1)

    def sup_lo(x):
        r = x % ROWS
        for k in range(2):
            dve.wait_ge(s.sup_hi, 2 * x + k + 1)
            nc.vector.tensor_tensor(sup_view(m)[:, 1, k, :, bass.ts(r, P)], bank(m, 6 + k).rearrange("p (c r) -> p c r", r=P),
                                    sup_view(m)[:, 0, k, :, bass.ts(r, P)].bitcast(F32), ALU.subtract).then_inc(s.sup_lo, 1)

    def measure(h, e):
        a, b = m.pair[:, 0, :], m.pair[:, 1, :]
        v = h * C + e
        dve.wait_ge(s.misi_out, v + 1)
        nc.vector.tensor_tensor(a, bank(m, 3 * (e % 2)), a, ALU.subtract).then_inc(s.mr_done, 1)
        dve.wait_ge(s.mr_done, v + 1)
        nc.vector.tensor_tensor(a, a, a, ALU.mult).then_inc(s.mr_sq, 1)
        dve.wait_ge(s.mr_sq, v + 1)
        dve.wait_ge(s.mi_sq, v + 1)
        nc.vector.tensor_tensor(a, a, b, ALU.add).then_inc(s.amp_sq, 1)
        dve.wait_ge(s.amp_hi, v + 1)
        nc.vector.tensor_tensor(m.a[:, 1, bass.ts(e, HALF)], a, m.a[:, 0, bass.ts(e, HALF)].bitcast(F32),
                                ALU.subtract).then_inc(s.amp_lo, 1)

    def post(h, k):
        z = m.raw.rearrange("p a w -> p (a w)")
        a, b = m.pair[:, 0, :], m.pair[:, 1, :]
        sums, sums_sq, mean, rstd = (bank(m, n) for n in (2, 3, 4, 5))
        for e in range(2 * k, 2 * k + 2) if k < 2 else ():
            v = h * C + e
            cols = bass.ts(e, HALF)
            dve.wait_ge(s.z_pre, v + 1)
            if e:
                dve.wait_ge(s.z_added, v)
                nc.vector.tensor_tensor(sums, sums, z[:, cols], ALU.add).then_inc(s.z_added, 1)
            else:
                nc.vector.tensor_copy(sums, z[:, cols]).then_inc(s.z_added, 1)
            dve.wait_ge(s.z_sq, v + 1)
            if e:
                dve.wait_ge(s.z_sq_added, v)
                nc.vector.tensor_tensor(sums_sq, sums_sq, a, ALU.add).then_inc(s.z_sq_added, 1)
            else:
                nc.vector.tensor_copy(sums_sq, a).then_inc(s.z_sq_added, 1)
        if k == 1:
            dve.wait_ge(s.z_added, C * (h + 1))
            dve.wait_ge(s.z_sq_added, C * (h + 1))
            nc.vector.tensor_copy(a, sums).then_inc(s.z_sums, 1)
            nc.vector.tensor_copy(b, sums_sq).then_inc(s.z_sums, 1)
        if k == 2:
            dve.wait_ge(s.z_mean_sq, h + 1)
            nc.vector.tensor_tensor(b, rstd, a, ALU.subtract).then_inc(s.z_var_raw, 1)
            dve.wait_ge(s.z_var_raw, h + 1)
            nc.vector.tensor_scalar(b, b, 0.0, LN_EPS, ALU.max, ALU.add).then_inc(s.z_var, 1)
            dve.wait_ge(s.z_std, h + 1)
            nc.vector.reciprocal(rstd, a).then_inc(s.z_rstd, 1)
            dve.wait_ge(s.z_rstd, h + 1)
        for e in range(C) if k == 2 else ():
            v = h * C + e
            cols = bass.ts(e, HALF)
            nc.vector.tensor_tensor(z[:, cols], z[:, cols], mean, ALU.subtract).then_inc(s.z_centred, 1)
            dve.wait_ge(s.z_centred, v + 1)
            nc.vector.tensor_tensor(z[:, cols], z[:, cols], rstd, ALU.mult).then_inc(s.z_scaled, 1)
        for e in range(C) if k == 3 else ():
            v = h * C + e
            cols = bass.ts(e, HALF)
            dve.wait_ge(s.z_hi, v + 1)
            nc.vector.tensor_tensor(m.a[:, 1, cols], z[:, cols], m.a[:, 0, cols].bitcast(F32), ALU.subtract).then_inc(s.z_lo, 1)

    def top(h, j):
        v = h * C + j
        t = m.top_x[:, j % 2, :]
        dve.wait_ge(s.topped, v + 1)
        dve.wait_ge(s.top_x_loaded[j % 2], 16 * (v // 2 + 1))
        nc.vector.tensor_tensor(t, bank(m, j % 2), t, ALU.add).then_inc(s.top_sum, 1)
        dve.wait_ge(s.h1_hi, v + 1)
        dve.wait_ge(s.top_sum, v + 1)
        nc.vector.scalar_tensor_tensor(out=m.h1[:, j % 2, 1, :], in0=t, scalar=0.0, in1=m.h1[:, j % 2, 0, :].bitcast(F32),
                                       op0=ALU.max, op1=ALU.subtract).then_inc(s.h1_lo, 1)

    def tile(x, part):
        units(2 * x)
        if x > ROWS:
            invert_norm(x - 1)
        cosines(2 * x)
        part(0, 0)
        directions(2 * x + 1)
        last_cosines(2 * x)
        superpose(2 * x)
        part(0, 1)
        if x > ROWS:
            sup_lo(x - 1)
        units(2 * x + 1)
        cosines(2 * x + 1)
        part(0, 2)
        if x + 1 < TILES:
            directions(2 * x + 2)
        last_cosines(2 * x + 1)
        superpose(2 * x + 1)
        part(0, 3)

    def nothing(h, k):
        pass

    dve.wait_ge(s.strength_loaded, 16 * TILES * N)
    for mat in range(4):
        cut(4 + mat, mat)
    for step in range(I_STEPS):
        x = step - N
        if x == 0:
            directions(0)
        take(step, 0)
        if x >= 0:
            units(2 * x)
        if x > 0:
            invert_norm(x - 1)
        if x >= 0:
            cosines(2 * x)
        take(step, 1)
        if step:
            cut(6 + 2 * step, 2 * ((step + 1) % 2))
        if x >= 0:
            directions(2 * x + 1)
            last_cosines(2 * x)
            superpose(2 * x)
        if step:
            cut(7 + 2 * step, 2 * ((step + 1) % 2) + 1)
        take(step, 2)
        if x > 0:
            sup_lo(x - 1)
        if x >= 0:
            units(2 * x + 1)
            cosines(2 * x + 1)
        take(step, 3)
        if x >= 0:
            if step + 1 < I_STEPS:
                directions(2 * x + 2)
            last_cosines(2 * x + 1)
            superpose(2 * x + 1)
    invert_norm(3)
    for mat in range(2):
        cut(22 + mat, 2 + mat)
    sup_lo(3)
    cut(24, 4, 1)
    directions(2 * ROWS)
    for x, part in ((4, measure), (5, post), (6, top), (7, nothing)):
        tile(x, part)
    invert_norm(7)
    sup_lo(7)
    for part in (measure, post, top):
        for k in range(4):
            part(1, k)


def final_pool(nc, pool, io, m, s):
    def store(k):
        step, k4 = divmod(k, 4)
        half, n = divmod(step, N)
        pool.wait_ge(s.r_done, k + 1)
        pool.wait_ge(s.i_out, k + 1)
        pool.dma_start(io.ri_scr[half * ROWS + k4, :, n, :], m.stage[:, k % 2, :]).then_inc(s.ri_stored[k % 2], 16)

    def load(y):
        x, b = divmod(y, 2)
        if x % ROWS == 0:
            for e in range(2):
                pool.wait_ge(s.ri_stored[e], 16 * (I_TILES // 4) * (x // ROWS + 1))
        if y >= 2:
            pool.wait_ge(s.fz_done, y - 1)
        src = io.ri_scr[x].rearrange("p n (k d) -> p (n k) d", k=2)[:, :, bass.ts(b, W)]
        pool.dma_start(m.ri[:, b, :].rearrange("p (a d) -> p a d", d=W), src).then_inc(s.ri_loaded[b], 16)

    def zeros(y):
        pool.wait_ge(s.x_sum, y + 1)
        if y:
            pool.wait_ge(s.zero_pairs, 6 * y)
        nc.gpsimd.tensor_scalar(m.zero[:, :], m.n2[:, y % 2, :], 0.0, None, ALU.is_equal).then_inc(s.x_zero, 1)

    def add_zeros(y):
        pool.wait_ge(s.x_zero, y + 1)
        pool.wait_ge(s.x_step, y + 1)
        pool.wait_ge(s.x_guess_sq, y + 1)
        zero = m.zero[:, :].rearrange("p (n d) -> p n d", n=N)
        for n, (i, j) in enumerate(PAIRS_OF_N):
            nc.gpsimd.tensor_tensor(zero_sums(m, y)[:, n], zero[:, i], zero[:, j], ALU.add).then_inc(s.zero_pairs, 1)

    def add_up(y):
        x, b = divmod(y, 2)
        u = m.u[:, b, :]
        pool.wait_ge(s.fz_done, y + 1)
        nc.gpsimd.tensor_tensor(u[:, 0:4 * W], u[:, 0:4 * W], u[:, 4 * W:8 * W], ALU.add).then_inc(s.half_sum, 1)
        pool.wait_ge(s.half_sum, y + 1)
        if x and b == 0:
            pool.wait_ge(s.turned, 2 * x)
        halves = u[:, 0:4 * W].rearrange("p (n k d) -> p n k d", n=2, k=2)
        nc.gpsimd.tensor_tensor(m.sup[:, :, bass.ts(b, W)], halves[:, 0], halves[:, 1], ALU.add).then_inc(s.sup_sum, 1)

    def load_mean(h):
        pool.dma_start(m.top_x[:, 0, 0:P], io.mean_of_out).then_inc(s.mean_loaded, 16)
        pool.wait_ge(s.mean_loaded, 16 * (h + 1))
        nc.gpsimd.tensor_copy(m.mean_of_out, m.top_x[:, 0, 0:P]).then_inc(s.mean_ready, 1)
        pool.wait_ge(s.mean_ready, h + 1)

    def load_top(h, j):
        v = h * C + j
        if v >= 2:
            pool.wait_ge(s.h1_lo, v - 1)
        if h and j == 0:
            pool.wait_ge(s.y_stored, 16)
            load_mean(h)
        pool.dma_start(m.top_x[:, j % 2, :], io.top_scr[j, :, bass.ts(h, HALF)]).then_inc(s.top_x_loaded[j % 2], 16)

    pool.wait_ge(s.attn_done, 2 * C * TILES)
    pool.wait_ge(s.stored_top, 16 * C * HALVES)
    for k in range(I_TILES):
        if k == I_TILES // 2:
            load(0)
            load(1)
        store(k)
        y = (k - I_TILES // 2) // 2
        if k == I_TILES // 2:
            zeros(0)
        if y >= 0 and k % 2 == 0:
            add_zeros(y)
        if y >= 0 and k % 2 == 1:
            if y + 1 < 2 * ROWS:
                zeros(y + 1)
            if y + 2 < 2 * ROWS:
                load(y + 2)
            add_up(y)
    load(2 * ROWS)
    load(2 * ROWS + 1)
    load_mean(0)
    for j in range(2):
        load_top(0, j)
    zeros(2 * ROWS)
    for y in range(2 * ROWS, 2 * TILES):
        add_zeros(y)
        if y == 2 * TILES - 3:
            load_top(0, 3)
        if y + 1 < 2 * TILES:
            zeros(y + 1)
        if y + 2 < 2 * TILES:
            load(y + 2)
        add_up(y)
        if y == 2 * TILES - 4:
            load_top(0, 2)
    for j in range(C):
        load_top(1, j)




def gather_strengths(nc, pool, io, m, s):
    pool.dma_start(m.ids[:, :], io.ids).then_inc(s.ids_loaded, 16)
    pool.wait_ge(s.ids_loaded, 16)
    for x in range(TILES):
        for f, table in enumerate(io.tables):
            nc.gpsimd.indirect_dma_start(
                out=m.strength[:, x, N * f:N * f + N], out_offset=None, in_=table,
                in_offset=bass.IndirectOffsetOnAxis(ap=m.ids[:, x * N + f:x * N + f + 1], axis=0),
            ).then_inc(s.strength_loaded, 16)


LATE_DMAS = 3


class Names:
    pass


def name_semaphores(nc, ctx):
    s = Names()

    def one(name):
        return ctx.enter_context(nc.semaphore(name))

    def two(name):
        return [one(name + "0"), one(name + "1")]

    s.aiwi_out = one("aiwi_out")
    s.amp_hi = one("amp_hi")
    s.amp_lo = one("amp_lo")
    s.amp_root = one("amp_root")
    s.amp_sq = one("amp_sq")
    s.at_hi = one("at_hi")
    s.at_lo = one("at_lo")
    s.at_stored = two("at_stored")
    s.attn_done = one("attn_done")
    s.bias_done = one("bias_done")
    s.block_done = one("block_done")
    s.bo_done = one("bo_done")
    s.bv_done = one("bv_done")
    s.compacted = one("compacted")
    s.consts_loaded = one("consts_loaded")
    s.cos_done = one("cos_done")
    s.evac_act = one("evac_act")
    s.evac_dve = one("evac_dve")
    s.exp_done = one("exp_done")
    s.f_done = one("f_done")
    s.f_first = one("f_first")
    s.fz_done = one("fz_done")
    s.gathered = one("gathered")
    s.gelu_done = one("gelu_done")
    s.h1_hi = one("h1_hi")
    s.h1_lo = one("h1_lo")
    s.h2_done = one("h2_done")
    s.h2_part = one("h2_part")
    s.half_sum = one("half_sum")
    s.hi_done = one("hi_done")
    s.i_done = one("i_done")
    s.i_out = one("i_out")
    s.ids_loaded = one("ids_loaded")
    s.inverse_done = one("inverse_done")
    s.late_loaded = one("late_loaded")
    s.lo_done = one("lo_done")
    s.mag2_done = one("mag2_done")
    s.mag_done = one("mag_done")
    s.masked = one("masked")
    s.max_done = one("max_done")
    s.mean_loaded = one("mean_loaded")
    s.mean_ready = one("mean_ready")
    s.mean_sq = one("mean_sq")
    s.means_done = one("means_done")
    s.measured = one("measured")
    s.mi_sq = one("mi_sq")
    s.misi_out = one("misi_out")
    s.mr_done = one("mr_done")
    s.mr_sq = one("mr_sq")
    s.nki_done = one("nki_done")
    s.norm_centred = one("norm_centred")
    s.norm_hi = one("norm_hi")
    s.norm_inverse = one("norm_inverse")
    s.norm_lo = one("norm_lo")
    s.norm_root = one("norm_root")
    s.norm_scaled = one("norm_scaled")
    s.norm_sum = one("norm_sum")
    s.ot_hi = one("ot_hi")
    s.ot_lo = one("ot_lo")
    s.pair_mul = one("pair_mul")
    s.pair_sum = one("pair_sum")
    s.posted = one("posted")
    s.pre_added = one("pre_added")
    s.pre_done = one("pre_done")
    s.projected = one("projected")
    s.qk_hi = one("qk_hi")
    s.qk_lo = one("qk_lo")
    s.quarter_loaded = two("quarter_loaded")
    s.r_done = one("r_done")
    s.raw_loaded = two("raw_loaded")
    s.ri_loaded = two("ri_loaded")
    s.ri_stored = two("ri_stored")
    s.rstd_done = one("rstd_done")
    s.scored = one("scored")
    s.shifted = one("shifted")
    s.softmaxed = one("softmaxed")
    s.spread_done = one("spread_done")
    s.sq_added = one("sq_added")
    s.sq_done = one("sq_done")
    s.std_done = one("std_done")
    s.stored = one("stored")
    s.stored_top = one("stored_top")
    s.strength_loaded = one("strength_loaded")
    s.sums_ready = one("sums_ready")
    s.sup_done = one("sup_done")
    s.sup_hi = one("sup_hi")
    s.sup_lo = one("sup_lo")
    s.sup_sum = one("sup_sum")
    s.table_loaded = one("table_loaded")
    s.tile_loaded = two("tile_loaded")
    s.top_sum = one("top_sum")
    s.top_x_loaded = two("top_x_loaded")
    s.topped = one("topped")
    s.total_done = one("total_done")
    s.turned = one("turned")
    s.u_done = one("u_done")
    s.v_done = one("v_done")
    s.v_hi = one("v_hi")
    s.v_lo = one("v_lo")
    s.v_tile_loaded = one("v_tile_loaded")
    s.var_done = one("var_done")
    s.var_raw = one("var_raw")
    s.weighed = one("weighed")
    s.wf_hi = one("wf_hi")
    s.wf_lo = one("wf_lo")
    s.wt_done = one("wt_done")
    s.wt_hi = one("wt_hi")
    s.wt_lo = one("wt_lo")
    s.x_guess = one("x_guess")
    s.x_guess_sq = one("x_guess_sq")
    s.x_inverse = one("x_inverse")
    s.x_ln = one("x_ln")
    s.x_sq = one("x_sq")
    s.x_step = one("x_step")
    s.x_sum = one("x_sum")
    s.x_zero = one("x_zero")
    s.y_done = one("y_done")
    s.y_out = one("y_out")
    s.y_stored = one("y_stored")
    s.z_added = one("z_added")
    s.z_centred = one("z_centred")
    s.z_gelu = one("z_gelu")
    s.z_hi = one("z_hi")
    s.z_lo = one("z_lo")
    s.z_mean_sq = one("z_mean_sq")
    s.z_means = one("z_means")
    s.z_pre = one("z_pre")
    s.z_rstd = one("z_rstd")
    s.z_scaled = one("z_scaled")
    s.z_sq = one("z_sq")
    s.z_sq_added = one("z_sq_added")
    s.z_std = one("z_std")
    s.z_sums = one("z_sums")
    s.z_var = one("z_var")
    s.z_var_raw = one("z_var_raw")
    s.zero_pairs = one("zero_pairs")
    return s




def place_memory(nc, ctx):
    m = Names()

    def sb(shape, name, dt=F32, stack=ctx):
        return stack.enter_context(nc.sbuf_tensor(name, shape, dt))

    m.x = sb([P, 2, KC * HALF], "x", F32R)
    m.h = sb([P, 2, KC * HALF], "h", F32R)
    m.params = sb([P, PARAMS], "params")
    m.table = sb([P, P], "table")
    m.strength = sb([P, TILES, N * N], "strength")
    m.raw = sb([P, 2, UNIT], "raw")
    with ExitStack() as e:
        m.pre = sb([P, KC * HALF], "pre", stack=e)
        m.ws = sb([P, 2, 2, 2, UNIT], "ws", F32R, e)
        m.tmp = sb([P, 2, HALF], "tmp", stack=e)
        m.ids = sb([P, TILES * N], "ids", I32, e)
    with ExitStack() as qv:
        m.weights = sb([P, TILES * P], "weights", stack=qv)
        m.own_row = sb([P, 32], "own_row", stack=qv)
        m.own_n = sb([P, N], "own_n", stack=qv)
        m.select = sb([P, N, P], "select", stack=qv)
        with ExitStack() as q:
            m.qk = sb([P, QK_BUFS, 5, 2, 512], "qk", F32R, q)
            m.masked = sb([P, 4, 512], "masked", stack=q)
            m.compact = sb([P, PAIRS, 2, 2, 16], "compact", stack=q)
            m.squares = sb([P, 256], "squares", stack=q)
            m.mag2 = sb([P, P], "mag2", stack=q)
            m.mag = sb([P, P], "mag", stack=q)
            m.top = sb([P, 32], "top", stack=q)
            m.total = sb([P, 32], "total", stack=q)
            m.inverse = sb([P, 32], "inverse", stack=q)
        with ExitStack() as v:
            m.v = sb([P, 2, 2, 2, D], "v", F32R, v)
            m.wf = sb([P, 2, HEADS * P], "wf", F32R, v)
            m.ot = sb([P, 2, 2, PAIRS, 512], "ot", F32R, v)
            m.wt = sb([P, 2, P], "wt", F32R, v)
            m.spread = sb([P, N, P], "spread", stack=v)
            m.bv = sb([P, 2, PAIRS, 2], "bv", F32R, v)
            m.bo = sb([P, 2 * C], "bo", stack=v)
    m.ri = sb([P, 2, 2 * N * W], "ri")
    m.u = sb([P, 2, 2 * N * W], "u")
    m.sq = sb([P, 2, 2 * N * W], "sq")
    m.n2 = sb([P, 2, N * W], "n2")
    m.zero = sb([P, N * W], "zero", BF16)
    m.sup = sb([P, 2, D], "sup")
    m.norms = sb([P, 3], "norms")
    with ExitStack() as i:
        m.stage = sb([P, 2, 1024], "stage", stack=i)
    m.top_x = sb([P, 2, HALF], "top_x")
    m.pair = sb([P, 2, HALF], "pair")
    m.a = m.h[:, 0, 0:4096].rearrange("p (b w) -> p b w", b=2)
    m.h1 = m.h[:, 0, 4096:6144].rearrange("p (k b w) -> p k b w", k=2, b=2)
    m.mean_of_out = m.h[:, 0, 4096:4096 + P]
    m.top2 = m.h[:, 0, 6144:8192].rearrange("p (b w) -> p b w", b=2)
    m.acc = ctx.enter_context(nc.psum_tensor("acc", [P, 4, 512], F32))
    m.stat = ctx.enter_context(nc.psum_tensor("stat", [P, 4, 512], F32))
    m.mean, m.rstd, m.sums, m.sums_sq = (m.stat[:, i, :] for i in range(4))
    return m


def program(nc, io):
    with ExitStack() as ctx:
        m, s = place_memory(nc, ctx), name_semaphores(nc, ctx)
        block = ctx.enter_context(nc.Block())

        @block.sync
        def _(sp):
            encoder_loads(nc, sp, io, m, s)
            scores_sync(nc, sp, io, m, s)
            values_sync(nc, sp, io, m, s)
            final_sync(nc, sp, io, m, s)

        @block.scalar
        def _(act):
            act.dma_start(m.params[:, :], io.params).then_inc(s.consts_loaded, 16)
            act.dma_start(m.table[:, :], io.mean_of_hid).then_inc(s.consts_loaded, 16)
            act.wait_ge(s.consts_loaded, 32)
            encoder_scalar(nc, act, io, m, s)
            qk_scalar(nc, act, io, m, s)
            values_scalar(nc, act, io, m, s)
            final_scalar(nc, act, io, m, s)

        @block.vector
        def _(dve):
            dve.wait_ge(s.consts_loaded, 32)
            encoder_vector(nc, dve, io, m, s)
            qk_vector(nc, dve, io, m, s)
            values_vector(nc, dve, io, m, s)
            final_vector(nc, dve, io, m, s)

        @block.tensor
        def _(pe):
            pe.wait_ge(s.consts_loaded, 32)
            encoder_tensor(nc, pe, io, m, s)
            scores_tensor(nc, pe, io, m, s)
            values_tensor(nc, pe, io, m, s)
            pe.wait_ge(s.table_loaded, 16)
            final_tensor(nc, pe, io, m, s)

        @block.gpsimd
        def _(pool):
            gather_strengths(nc, pool, io, m, s)
            encoder_stores(nc, pool, io, m, s)
            pool.wait_ge(s.strength_loaded, 16 * TILES * N)
            pool.wait_ge(s.norm_lo, 32 * HALVES)
            pool.dma_start(m.own_row[:, :], io.own_row).then_inc(s.late_loaded, 16)
            pool.dma_start(m.own_n[:, :], io.own_n).then_inc(s.late_loaded, 16)
            pool.dma_start(m.select[:, :, :], io.select).then_inc(s.late_loaded, 16)
            pool.wait_ge(s.means_done, 2 * HALVES)
            pool.dma_start(m.table[:, :], io.identity).then_inc(s.table_loaded, 16)
            values_pool(nc, pool, io, m, s)
            final_pool(nc, pool, io, m, s)



def kernel(**inputs):
    import numpy as _np
    import concourse.bacc as _bacc
    from concourse import mybir as _mybir
    from concourse.bass_utils import run_bass_kernel_spmd as _run

    nc = _bacc.Bacc("TRN2", target_bir_lowering=False, num_devices=1)
    arrays, io = {}, Names()
    given = {k.replace("L0_rec_", ""): _np.asarray(v) for k, v in inputs.items()}

    def give(name, array):
        array = _np.ascontiguousarray(array)
        arrays["in_" + name] = array
        return nc.dram_tensor("in_" + name, array.shape, _mybir.dt.from_np(array.dtype), kind="ExternalInput").ap()

    def scratch(name, shape):
        return nc.dram_tensor(name, shape, _mybir.dt.float32, kind="Internal").ap()

    def narrow(w):
        k, n = w.shape
        return w.reshape(k // UNIT, UC, P, n // P, P).transpose(3, 0, 2, 1, 4).reshape(-1, P, UNIT)

    def wide(w):
        return w.reshape(C, P, -1).transpose(1, 0, 2).reshape(P, -1, UNIT).transpose(1, 0, 2)

    x = given["r_x"].T
    x_halves = [x[:, k * HALF:(k + 1) * HALF].reshape(X_UNITS, 2, P, HALF).transpose(0, 2, 1, 3).reshape(X_UNITS, P, UNIT)
                for k in range(HALVES)]
    z_features = D
    io.w_units = give("w_units", _np.concatenate([narrow(given[k].T) for k in ("er_W1", "ei_W1", "er_W2", "ei_W2")]
                                    + [narrow(given["W_top1"][z_features:])]))
    io.x_units = give("x_units", _np.concatenate(x_halves + [wide(given[k].T) for k in ("Wq_r", "Wq_i", "Wk_r", "Wk_i")]))
    late = [given[k].T for k in ("Wv_r", "Wv_i", "Wo_r", "Wo_i")]
    for n in range(N):
        late += [given["int_Wr"][n].T, given["int_Wi"][n].T]
    late += [given["meas_Mr"].T, given["meas_Mi"].T, given["post_W"].T, given["W_top1"][:z_features], given["W_top2"]]
    io.late_units = give("late_units", _np.concatenate([wide(w) for w in late]))
    columns = ("er_b1", "er_g1", "er_be1", "ei_b1", "ei_g1", "ei_be1", "er_b2", "ei_b2", "b_top1", "bq_r", "bq_i", "bk_r",
               "bk_i", "bv_r", "bv_i", "bo_r", "bo_i", "post_b", "post_g", "post_be", "b_top2", "W_top3")
    io.params = give("params", _np.concatenate([given[k].reshape(-1, P).T for k in columns] + [_np.full((P, 1), k, _np.float32) for k in (TINY, 1e-8)], axis=1))
    io.ids = give("ids", given["ids"].reshape(TILES, P, N).transpose(1, 0, 2).reshape(P, TILES * N))
    io.tables = [give("tbl_" + str(f), given["tbl_" + str(f)]) for f in range(N)]
    p = _np.arange(P)
    f32 = _np.float32
    io.mean_of_hid = give("mean_of_hid", _np.full((P, P), 1.0 / HID, f32))
    io.mean_of_out = give("mean_of_out", _np.full((P, P), 1.0 / D, f32))
    io.identity = give("identity", _np.eye(P, dtype=f32))
    io.own_row = give("own_row", (p[:, None] % 32 == _np.arange(32)).astype(f32))
    io.own_n = give("own_n", (p[:, None] // 32 == _np.arange(N)).astype(f32))
    io.select = give("select", ((p[:, None, None] % 32 == p % 32) & (p // 32 == _np.arange(N)[:, None])).astype(f32))
    io.s_scr = scratch("s_scr", (2, 2, N, C, P, BATCH))
    io.top_scr = scratch("top_scr", (C, P, BATCH))
    io.a_scr = scratch("a_scr", (2, 2, N, C, P, BATCH))
    io.ri_scr = scratch("ri_scr", (TILES, P, N, 2 * D))
    io.y = nc.dram_tensor("out_y", (HALVES, HALF), _mybir.dt.float32, kind="ExternalOutput").ap()
    program(nc, io)
    result = _run(nc, [arrays], core_ids=[0])
    return result.results[0]["out_y"].reshape(BATCH, 1)
```
